# Optimizing a Trainium2 kernel written in Bass

```python
import numpy as np
import jax
import jax.numpy as jnp

def _softmax(x, axis=-1):
    return jax.nn.softmax(x, axis=axis)

def _gelu(x):
    return jax.nn.gelu(x, approximate=True)

def _silu(x):
    return jax.nn.silu(x)

def _sigmoid(x):
    return jax.nn.sigmoid(x)

def _layernorm(x, axis=-1, eps=1e-05):
    m = jnp.mean(x, axis=axis, keepdims=True)
    v = jnp.var(x, axis=axis, keepdims=True)
    return (x - m) / jnp.sqrt(v + eps)

def _scatter_add(tgt, idx, src, axis=0):
    return tgt.at[idx].add(src)

def _segment_sum(src, seg, n):
    return jax.ops.segment_sum(src, seg, n)
kernel_name = 'mk_vit_tower_d1_tok_img512_r4_5cf681'

def setup_inputs(seed: int=0):
    np.random.seed(seed)
    _w = jnp.asarray

    def _rec_inputs():
        import jax
        import jax.numpy as jnp
        _rk = jax.random.key(seed)
        x = 7.57192e-06 + 1.00007 * jax.random.normal(jax.random.fold_in(_rk, 1), (64, 3, 224, 224), jnp.float32)
        return x
    x = _rec_inputs()

    def _L0_tok_setup():
        import jax, jax.numpy as jnp
        import numpy as np
        DEPTH = 4
        HEADS = 8
        DIM = 128
        HID = 256
        P = 16
        IMG = 224
        GRID = IMG // P
        NPATCH = GRID * GRID
        NTOK = NPATCH + 1
        BATCH = 64
        EPS = 1e-05

        def layernorm(x, w, b):
            mu = jnp.mean(x, axis=-1, keepdims=True)
            var = jnp.mean(jnp.square(x - mu), axis=-1, keepdims=True)
            return (x - mu) * jax.lax.rsqrt(var + EPS) * w + b
        key = jax.random.key(seed)
        ks = jax.random.split(key, 12)
        s = 0.02
        inp = {'x': jax.random.normal(ks[0], (BATCH, 3, IMG, IMG), jnp.float32), 'conv_w': jax.random.normal(ks[1], (3 * P * P, DIM), jnp.float32) * s, 'conv_b': jnp.zeros((DIM,), jnp.float32), 'cls_token': jax.random.normal(ks[2], (1, 1, DIM), jnp.float32) * s, 'pos_embed': jax.random.normal(ks[3], (1, NTOK, DIM), jnp.float32) * s, 'ln1_w': jnp.ones((DEPTH, DIM), jnp.float32), 'ln1_b': jnp.zeros((DEPTH, DIM), jnp.float32), 'qkv_w': jax.random.normal(ks[4], (DEPTH, DIM, 3 * DIM), jnp.float32) * s, 'qkv_b': jnp.zeros((DEPTH, 3 * DIM), jnp.float32), 'proj_w': jax.random.normal(ks[5], (DEPTH, DIM, DIM), jnp.float32) * s, 'proj_b': jnp.zeros((DEPTH, DIM), jnp.float32), 'ln2_w': jnp.ones((DEPTH, DIM), jnp.float32), 'ln2_b': jnp.zeros((DEPTH, DIM), jnp.float32), 'fc1_w': jax.random.normal(ks[6], (DEPTH, DIM, HID), jnp.float32) * s, 'fc1_b': jnp.zeros((DEPTH, HID), jnp.float32), 'fc2_w': jax.random.normal(ks[7], (DEPTH, HID, DIM), jnp.float32) * s, 'fc2_b': jnp.zeros((DEPTH, DIM), jnp.float32), 'norm_w': jnp.ones((DIM,), jnp.float32), 'norm_b': jnp.zeros((DIM,), jnp.float32)}
        return inp
    _L0_tok_all = _L0_tok_setup()
    _L0_tok_in = {k: v for k, v in _L0_tok_all.items() if k in ('conv_w', 'conv_b', 'cls_token', 'pos_embed', 'ln1_w', 'ln1_b', 'qkv_w', 'qkv_b', 'proj_w', 'proj_b', 'ln2_w', 'ln2_b', 'fc1_w', 'fc1_b', 'fc2_w', 'fc2_b', 'norm_w', 'norm_b')}
    del _L0_tok_all

    def _L0_attn_setup():
        import jax, jax.numpy as jnp
        import numpy as np
        B, T, D = (4, 1024, 128)
        STD = 0.02
        key = jax.random.key(seed)
        ks = jax.random.split(key, 7)
        x = jax.random.normal(ks[0], (B, T, D), dtype=jnp.float32)
        Wq = STD * jax.random.normal(ks[1], (D, D), dtype=jnp.float32)
        Wk = STD * jax.random.normal(ks[2], (D, D), dtype=jnp.float32)
        Wv = STD * jax.random.normal(ks[3], (D, D), dtype=jnp.float32)
        Wo = STD * jax.random.normal(ks[4], (D, D), dtype=jnp.float32)
        decay_logit = jnp.asarray(3.0, dtype=jnp.float32)
        out_scale = jnp.asarray(0.1, dtype=jnp.float32)
        return {'x': x, 'Wq': Wq, 'Wk': Wk, 'Wv': Wv, 'Wo': Wo, 'decay_logit': decay_logit, 'out_scale': out_scale}
    _L0_attn_all = _L0_attn_setup()
    _L0_attn_in = {k: v for k, v in _L0_attn_all.items() if k in ('Wq', 'Wk', 'Wv', 'Wo', 'decay_logit', 'out_scale')}
    del _L0_attn_all

    def _L0_ffn_setup():
        import jax, jax.numpy as jnp
        import numpy as np
        from functools import partial
        EPS = 1e-05
        ROPE_THETA = 10000.0
        TOP_K = 2

        def rmsnorm(x, w):
            var = jnp.mean(x * x, axis=-1, keepdims=True)
            return x * jax.lax.rsqrt(var + EPS) * w

        def apply_rope(x):
            B, S, H, dh = x.shape
            inv_freq = 1.0 / ROPE_THETA ** (jnp.arange(0, dh, 2, dtype=jnp.float32) / dh)
            ang = jnp.arange(S, dtype=jnp.float32)[:, None] * inv_freq[None, :]
            cos = jnp.cos(ang)[None, :, None, :]
            sin = jnp.sin(ang)[None, :, None, :]
            x1 = x[..., 0::2]
            x2 = x[..., 1::2]
            r1 = x1 * cos - x2 * sin
            r2 = x1 * sin + x2 * cos
            return jnp.stack([r1, r2], axis=-1).reshape(x.shape)

        def mha_rope(xn, wq, wk, wv, wo, num_heads):
            B, S, D = xn.shape
            dh = D // num_heads
            q = (xn @ wq).reshape(B, S, num_heads, dh)
            k = (xn @ wk).reshape(B, S, num_heads, dh)
            v = (xn @ wv).reshape(B, S, num_heads, dh)
            q = apply_rope(q)
            k = apply_rope(k)
            scores = jnp.einsum('bqhd,bkhd->bhqk', q, k) / jnp.sqrt(jnp.float32(dh))
            causal = jnp.tril(jnp.ones((S, S), dtype=bool))
            scores = jnp.where(causal[None, None], scores, jnp.float32(-1000000000.0))
            attn = jax.nn.softmax(scores, axis=-1)
            out = jnp.einsum('bhqk,bkhd->bqhd', attn, v).reshape(B, S, D)
            return out @ wo

        def moe_ffn(hn, router_w, w1, w2):
            B, S, D = hn.shape
            E = router_w.shape[1]
            t = hn.reshape(B * S, D)
            T = t.shape[0]
            logits = t @ router_w
            probs = jax.nn.softmax(logits, axis=-1)
            vals, idx = jax.lax.top_k(probs, TOP_K)
            gates = vals / jnp.sum(vals, axis=-1, keepdims=True)
            gates_dense = jnp.zeros((T, E), dtype=t.dtype).at[jnp.arange(T)[:, None], idx].add(gates)
            out = jnp.zeros_like(t)
            for e in range(E):
                ge = gates_dense[:, e:e + 1]
                h = jax.nn.gelu(t @ w1[e], approximate=False)
                out = out + ge * (h @ w2[e])
            return out.reshape(B, S, D)
        key = jax.random.key(seed)
        B, S, D, H, E = (4, 512, 128, 8, 8)
        Hf = 4 * D
        ks = jax.random.split(key, 10)
        s = 0.02
        return {'x': jax.random.normal(ks[0], (B, S, D), dtype=jnp.float32), 'attn_norm_w': jnp.ones((D,), dtype=jnp.float32), 'wq': jax.random.normal(ks[1], (D, D), dtype=jnp.float32) * s, 'wk': jax.random.normal(ks[2], (D, D), dtype=jnp.float32) * s, 'wv': jax.random.normal(ks[3], (D, D), dtype=jnp.float32) * s, 'wo': jax.random.normal(ks[4], (D, D), dtype=jnp.float32) * s, 'ffn_norm_w': jnp.ones((D,), dtype=jnp.float32), 'router_w': jax.random.normal(ks[5], (D, E), dtype=jnp.float32) * s, 'w1': jax.random.normal(ks[6], (E, D, Hf), dtype=jnp.float32) * s, 'w2': jax.random.normal(ks[7], (E, Hf, D), dtype=jnp.float32) * s}
    _L0_ffn_all = _L0_ffn_setup()
    _L0_ffn_in = {k: v for k, v in _L0_ffn_all.items() if k in ('attn_norm_w', 'wq', 'wk', 'wv', 'wo', 'ffn_norm_w', 'router_w', 'w1', 'w2')}
    del _L0_ffn_all
    return {'x': x, 'L0_tok_conv_w': _L0_tok_in['conv_w'], 'L0_tok_conv_b': _L0_tok_in['conv_b'], 'L0_tok_cls_token': _L0_tok_in['cls_token'], 'L0_tok_pos_embed': _L0_tok_in['pos_embed'], 'L0_tok_ln1_w': _L0_tok_in['ln1_w'], 'L0_tok_ln1_b': _L0_tok_in['ln1_b'], 'L0_tok_qkv_w': _L0_tok_in['qkv_w'], 'L0_tok_qkv_b': _L0_tok_in['qkv_b'], 'L0_tok_proj_w': _L0_tok_in['proj_w'], 'L0_tok_proj_b': _L0_tok_in['proj_b'], 'L0_tok_ln2_w': _L0_tok_in['ln2_w'], 'L0_tok_ln2_b': _L0_tok_in['ln2_b'], 'L0_tok_fc1_w': _L0_tok_in['fc1_w'], 'L0_tok_fc1_b': _L0_tok_in['fc1_b'], 'L0_tok_fc2_w': _L0_tok_in['fc2_w'], 'L0_tok_fc2_b': _L0_tok_in['fc2_b'], 'L0_tok_norm_w': _L0_tok_in['norm_w'], 'L0_tok_norm_b': _L0_tok_in['norm_b'], 'L0_attn_Wq': _L0_attn_in['Wq'], 'L0_attn_Wk': _L0_attn_in['Wk'], 'L0_attn_Wv': _L0_attn_in['Wv'], 'L0_attn_Wo': _L0_attn_in['Wo'], 'L0_attn_decay_logit': _L0_attn_in['decay_logit'], 'L0_attn_out_scale': _L0_attn_in['out_scale'], 'L0_ffn_attn_norm_w': _L0_ffn_in['attn_norm_w'], 'L0_ffn_wq': _L0_ffn_in['wq'], 'L0_ffn_wk': _L0_ffn_in['wk'], 'L0_ffn_wv': _L0_ffn_in['wv'], 'L0_ffn_wo': _L0_ffn_in['wo'], 'L0_ffn_ffn_norm_w': _L0_ffn_in['ffn_norm_w'], 'L0_ffn_router_w': _L0_ffn_in['router_w'], 'L0_ffn_w1': _L0_ffn_in['w1'], 'L0_ffn_w2': _L0_ffn_in['w2']}

def reference(x, L0_tok_conv_w, L0_tok_conv_b, L0_tok_cls_token, L0_tok_pos_embed, L0_tok_ln1_w, L0_tok_ln1_b, L0_tok_qkv_w, L0_tok_qkv_b, L0_tok_proj_w, L0_tok_proj_b, L0_tok_ln2_w, L0_tok_ln2_b, L0_tok_fc1_w, L0_tok_fc1_b, L0_tok_fc2_w, L0_tok_fc2_b, L0_tok_norm_w, L0_tok_norm_b, L0_attn_Wq, L0_attn_Wk, L0_attn_Wv, L0_attn_Wo, L0_attn_decay_logit, L0_attn_out_scale, L0_ffn_attn_norm_w, L0_ffn_wq, L0_ffn_wk, L0_ffn_wv, L0_ffn_wo, L0_ffn_ffn_norm_w, L0_ffn_router_w, L0_ffn_w1, L0_ffn_w2):
    import jax
    import jax.numpy as jnp

    def _L0_tok_ref(x, conv_w, conv_b, cls_token, pos_embed, ln1_w, ln1_b, qkv_w, qkv_b, proj_w, proj_b, ln2_w, ln2_b, fc1_w, fc1_b, fc2_w, fc2_b, norm_w, norm_b):
        import jax, jax.numpy as jnp
        import numpy as np
        DEPTH = 4
        HEADS = 8
        DIM = 128
        HID = 256
        P = 16
        IMG = 224
        GRID = IMG // P
        NPATCH = GRID * GRID
        NTOK = NPATCH + 1
        BATCH = 64
        EPS = 1e-05

        def layernorm(x, w, b):
            mu = jnp.mean(x, axis=-1, keepdims=True)
            var = jnp.mean(jnp.square(x - mu), axis=-1, keepdims=True)
            return (x - mu) * jax.lax.rsqrt(var + EPS) * w + b
        B = x.shape[0]
        hd = DIM // HEADS
        scale = hd ** (-0.5)
        patches = x.reshape(B, 3, GRID, P, GRID, P)
        patches = patches.transpose(0, 2, 4, 1, 3, 5).reshape(B, NPATCH, 3 * P * P)
        tok = patches @ conv_w + conv_b
        cls = jnp.broadcast_to(cls_token, (B, 1, DIM))
        h = jnp.concatenate([cls, tok], axis=1) + pos_embed
        for i in range(DEPTH):
            y = layernorm(h, ln1_w[i], ln1_b[i])
            qkv = (y @ qkv_w[i] + qkv_b[i]).reshape(B, NTOK, 3, HEADS, hd)
            qkv = qkv.transpose(2, 0, 3, 1, 4)
            q, k, v = (qkv[0], qkv[1], qkv[2])
            attn = jax.nn.softmax(jnp.einsum('bhnd,bhmd->bhnm', q, k) * scale, axis=-1)
            o = jnp.einsum('bhnm,bhmd->bhnd', attn, v)
            o = o.transpose(0, 2, 1, 3).reshape(B, NTOK, DIM)
            h = h + (o @ proj_w[i] + proj_b[i])
            y = layernorm(h, ln2_w[i], ln2_b[i])
            y = jax.nn.gelu(y @ fc1_w[i] + fc1_b[i], approximate=False)
            h = h + (y @ fc2_w[i] + fc2_b[i])
        return layernorm(h, norm_w, norm_b)

    def _L0_attn_ref(x, Wq, Wk, Wv, Wo, decay_logit, out_scale):
        import jax, jax.numpy as jnp
        import numpy as np
        B, T, D = (4, 1024, 128)
        STD = 0.02
        q = x @ Wq.T
        k = x @ Wk.T
        v = x @ Wv.T
        scores = jnp.einsum('btd,bsd->bts', q, k)
        decay = jax.nn.sigmoid(decay_logit)
        pos = jnp.arange(x.shape[1])
        diff = pos[None, :] - pos[:, None]
        expo = jnp.maximum(diff.astype(x.dtype) - 1.0, 0.0)
        weights = jnp.where(diff > 0, decay ** expo, jnp.zeros((), x.dtype))
        retrieved = jnp.einsum('bts,bsd->btd', scores * weights[None], v)
        return retrieved @ Wo.T * out_scale

    def _L0_ffn_ref(x, attn_norm_w, wq, wk, wv, wo, ffn_norm_w, router_w, w1, w2):
        import jax, jax.numpy as jnp
        import numpy as np
        from functools import partial
        EPS = 1e-05
        ROPE_THETA = 10000.0
        TOP_K = 2

        def rmsnorm(x, w):
            var = jnp.mean(x * x, axis=-1, keepdims=True)
            return x * jax.lax.rsqrt(var + EPS) * w

        def apply_rope(x):
            B, S, H, dh = x.shape
            inv_freq = 1.0 / ROPE_THETA ** (jnp.arange(0, dh, 2, dtype=jnp.float32) / dh)
            ang = jnp.arange(S, dtype=jnp.float32)[:, None] * inv_freq[None, :]
            cos = jnp.cos(ang)[None, :, None, :]
            sin = jnp.sin(ang)[None, :, None, :]
            x1 = x[..., 0::2]
            x2 = x[..., 1::2]
            r1 = x1 * cos - x2 * sin
            r2 = x1 * sin + x2 * cos
            return jnp.stack([r1, r2], axis=-1).reshape(x.shape)

        def mha_rope(xn, wq, wk, wv, wo, num_heads):
            B, S, D = xn.shape
            dh = D // num_heads
            q = (xn @ wq).reshape(B, S, num_heads, dh)
            k = (xn @ wk).reshape(B, S, num_heads, dh)
            v = (xn @ wv).reshape(B, S, num_heads, dh)
            q = apply_rope(q)
            k = apply_rope(k)
            scores = jnp.einsum('bqhd,bkhd->bhqk', q, k) / jnp.sqrt(jnp.float32(dh))
            causal = jnp.tril(jnp.ones((S, S), dtype=bool))
            scores = jnp.where(causal[None, None], scores, jnp.float32(-1000000000.0))
            attn = jax.nn.softmax(scores, axis=-1)
            out = jnp.einsum('bhqk,bkhd->bqhd', attn, v).reshape(B, S, D)
            return out @ wo

        def moe_ffn(hn, router_w, w1, w2):
            B, S, D = hn.shape
            E = router_w.shape[1]
            t = hn.reshape(B * S, D)
            T = t.shape[0]
            logits = t @ router_w
            probs = jax.nn.softmax(logits, axis=-1)
            vals, idx = jax.lax.top_k(probs, TOP_K)
            gates = vals / jnp.sum(vals, axis=-1, keepdims=True)
            gates_dense = jnp.zeros((T, E), dtype=t.dtype).at[jnp.arange(T)[:, None], idx].add(gates)
            out = jnp.zeros_like(t)
            for e in range(E):
                ge = gates_dense[:, e:e + 1]
                h = jax.nn.gelu(t @ w1[e], approximate=False)
                out = out + ge * (h @ w2[e])
            return out.reshape(B, S, D)
        num_heads = 8
        h = x + mha_rope(rmsnorm(x, attn_norm_w), wq, wk, wv, wo, num_heads)
        out = h + moe_ffn(rmsnorm(h, ffn_norm_w), router_w, w1, w2)
        return out
    h = _L0_tok_ref(x, L0_tok_conv_w, L0_tok_conv_b, L0_tok_cls_token, L0_tok_pos_embed, L0_tok_ln1_w, L0_tok_ln1_b, L0_tok_qkv_w, L0_tok_qkv_b, L0_tok_proj_w, L0_tok_proj_b, L0_tok_ln2_w, L0_tok_ln2_b, L0_tok_fc1_w, L0_tok_fc1_b, L0_tok_fc2_w, L0_tok_fc2_b, L0_tok_norm_w, L0_tok_norm_b)
    h = h + _L0_attn_ref(_layernorm(h, axis=-1), L0_attn_Wq, L0_attn_Wk, L0_attn_Wv, L0_attn_Wo, L0_attn_decay_logit, L0_attn_out_scale)
    h = h + _L0_ffn_ref(_layernorm(h, axis=-1), L0_ffn_attn_norm_w, L0_ffn_wq, L0_ffn_wk, L0_ffn_wv, L0_ffn_wo, L0_ffn_ffn_norm_w, L0_ffn_router_w, L0_ffn_w1, L0_ffn_w2)
    return h

_drawn_inputs = setup_inputs


def setup_inputs(seed=0):
    import zlib

    import numpy as np

    out = dict(_drawn_inputs(seed))
    spreads = {'L0_tok_conv_b': (0.0, 0.1),
     'L0_tok_ln1_w': (1.0, 0.6),
     'L0_tok_ln1_b': (0.0, 0.483),
     'L0_tok_qkv_b': (0.0, 0.1),
     'L0_tok_proj_b': (0.0, 0.1),
     'L0_tok_ln2_w': (1.0, 0.6),
     'L0_tok_ln2_b': (0.0, 0.662),
     'L0_tok_fc1_b': (0.0, 0.1),
     'L0_tok_fc2_b': (0.0, 0.1),
     'L0_tok_norm_w': (1.0, 0.2),
     'L0_tok_norm_b': (0.0, 0.1),
     'L0_ffn_attn_norm_w': (1.0, 0.6),
     'L0_ffn_ffn_norm_w': (1.0, 0.6)}
    factors = {'L0_tok_cls_token': 8.0,
     'L0_attn_Wq': 4.191,
     'L0_attn_Wk': 4.063,
     'L0_attn_Wv': 4.045,
     'L0_attn_Wo': 3.921,
     'L0_ffn_wq': 8.0,
     'L0_ffn_wk': 8.0,
     'L0_ffn_wv': 4.851,
     'L0_ffn_wo': 4.28,
     'L0_ffn_router_w': 3.515,
     'L0_ffn_w1': 3.12,
     'L0_ffn_w2': 3.025}
    for name, (base, spread) in spreads.items():
        noise = np.random.default_rng([zlib.crc32(name.encode()), seed]).standard_normal(out[name].shape)
        drawn = base * np.exp(spread * noise) if base else spread * noise
        out[name] = jnp.asarray(drawn.astype(out[name].dtype))
    for name, factor in factors.items():
        out[name] = (out[name] * factor).astype(out[name].dtype)
    return out
```

```python
from contextlib import ExitStack

import numpy as np

import concourse.bass as bass
from concourse import mybir

F32 = mybir.dt.float32
F32R = mybir.dt.float32r
I32 = mybir.dt.int32
U32 = mybir.dt.uint32
ACT = mybir.ActivationFunctionType
ALU = mybir.AluOpType
AX = mybir.AxisListType.X

P = 128
D = 128
B = 64
IMG = 224
PATCH = 16
GRID = IMG // PATCH
NTOK = GRID * GRID + 1
NPAD = NTOK + 1
TILES = ((0, P), (P, NTOK - P))
LAYERS = 4
HEADS = 8
HD = D // HEADS
STRIP = 32
NSTRIP = P // STRIP
NGRP = HEADS // NSTRIP
GW = NGRP * NPAD
HID = 256
HC = HID // P
EXPERTS = 8
FF = 512
FC = FF // P
EPS = 1e-5
SCALE = HD ** -0.5
SLOTS = (0, 1)
PAIRS = B // 2
HALF = PATCH // 2
XROWS = 3 * PATCH
XSHIFT = 64
MASKED = -1.0e30

A_WQ = 0
A_WK = A_WQ + NGRP * P
A_WV = A_WK + NGRP * P
A_WP = A_WV + D
A_BV = A_WP + D
A_BP = A_BV + D
A_COL = A_BP + D
A_N = A_COL + 6
M_W1 = 0
M_W2 = M_W1 + HID
M_B2 = M_W2 + HC * D
M_COL = M_B2 + D
M_N = M_COL + 4
C_CONV = 0
C_FWQ = C_CONV + HALF * D
C_FWQS = C_FWQ + NGRP * P
C_FWK = C_FWQS + NGRP * P
C_FWKS = C_FWK + NGRP * P
C_FWV = C_FWKS + NGRP * P
C_FWO = C_FWV + D
C_RQ = C_FWO + D
C_RK = C_RQ + D
C_RV = C_RK + D
C_RO = C_RV + D
C_ROUT = C_RO + D
C_NW = C_ROUT + EXPERTS
C_NB = C_NW + D
C_POS = C_NB + D
C_COS = C_POS + NTOK
C_SIN = C_COS + GW
C_ONE = C_SIN + GW
C_ZERO = C_ONE + 1
C_FW1 = C_ZERO + 1
C_FW2 = C_FW1 + 1
C_CONVB = C_FW2 + 1
C_CLS = C_CONVB + 1
C_DECAY = C_CLS + 1
C_SCALE = C_DECAY + 1
C_N = C_SCALE + 1

NORMS = 2 * LAYERS + 5
TURNS = 2 * LAYERS + 3
ATTNS = LAYERS + 1


def build(nc, x, attn_w, mlp_w, const_w, w1, w2, out):
    with ExitStack() as ctx:
        def sb(name, shape, dt=F32):
            return ctx.enter_context(nc.sbuf_tensor(name, shape, dt))

        def pair_sb(name, shape, dt=F32):
            return [sb(f"{name}{s}", shape, dt) for s in SLOTS]

        def sem(name):
            return ctx.enter_context(nc.semaphore(name))

        def pair_sem(name):
            return [sem(f"{name}{s}") for s in SLOTS]

        aw = sb("aw", [P, A_N])
        mw = sb("mw", [P, M_N])
        cw = sb("cw", [P, C_N])
        up_w = [sb(f"up_w{j}", [P, FF]) for j in range(2)]
        down_w = [sb(f"down_w{j}", [P, FC, D]) for j in range(2)]
        ident = sb("ident", [P, P])
        ident_r = sb("ident_r", [P, P], F32R)
        causal_r = sb("causal_r", [P, 2, NPAD], F32R)
        causal = sb("causal", [P, 2, NPAD])
        den_ones = sb("den_ones", [P, NGRP, STRIP])
        decay_t = sb("decay_t", [P, 2, NPAD])
        expo_i = sb("expo_i", [P, 2, NPAD], I32)
        expert_i = sb("expert_i", [P, EXPERTS], I32)
        expert_f = sb("expert_f", [P, EXPERTS])
        mhalf = sb("mhalf", [P, 2])
        eps2 = sb("eps2", [P, 2])
        carrier = sb("carrier", [P, 5])
        posT = sb("posT", [P, NTOK])
        lnd = sb("lnd", [P, 6])

        img = pair_sb("img", [P, GRID, IMG])
        h = pair_sb("h", [P, 2, D])
        hh = pair_sb("hh", [P, 2, D])
        yn = pair_sb("yn", [P, 2, D])
        yT = pair_sb("yT", [P, NPAD])
        stats = pair_sb("stats", [P, 2, 6])
        mv = pair_sb("mv", [P, 2, 2])
        ve = pair_sb("ve", [P, 2])
        rstd = pair_sb("rstd", [P, 2])
        q_hi = pair_sb("q_hi", [P, NGRP, NPAD], F32R)
        q_lo = pair_sb("q_lo", [P, NGRP, NPAD], F32R)
        k_hi = pair_sb("k_hi", [P, NGRP, NPAD], F32R)
        k_lo = pair_sb("k_lo", [P, NGRP, NPAD], F32R)
        q_rot = pair_sb("q_rot", [P, GW])
        k_rot = pair_sb("k_rot", [P, GW])
        rot = pair_sb("rot", [P, 2, GW])
        vpad = pair_sb("vpad", [P, 2, NSTRIP, NGRP, STRIP])
        neg_max = pair_sb("neg_max", [P, 2, NGRP, P], F32R)
        prob = pair_sb("prob", [P, 2, NSTRIP, GW])
        rden = pair_sb("rden", [P, NTOK])
        oT = pair_sb("oT", [P, NTOK])
        gT = pair_sb("gT", [P, 2, GW])
        rkv = pair_sb("rkv", [P, 2, D])
        logit = pair_sb("logit", [P, 2, EXPERTS])
        top = pair_sb("top", [P, 2, EXPERTS])
        topi = pair_sb("topi", [P, 2, EXPERTS], U32)
        topf = pair_sb("topf", [P, 2, 2])
        gap = pair_sb("gap", [P, 2])
        second = pair_sb("second", [P, 2])
        den = pair_sb("den", [P, 2])
        gate = pair_sb("gate", [P, 2, 2])
        gates = pair_sb("gates", [P, 2, EXPERTS])
        gates2 = pair_sb("gates2", [P, 2, EXPERTS])

        psum = ctx.enter_context(nc.psum_tensor("psum", [P, 8, 512], F32))

        def bank(s, j):
            return psum[:, 4 * s + j, :]

        const_loaded = sem("const_loaded")
        attn_w_loaded = sem("attn_w_loaded")
        mlp_w_loaded = sem("mlp_w_loaded")
        expert_loaded = [sem(f"expert_loaded{j}") for j in range(2)]
        img_loaded = pair_sem("img_loaded")
        h_free = pair_sem("h_free")
        pool_set = sem("pool_set")
        dve_set = sem("dve_set")
        act_set = sem("act_set")
        patches = pair_sem("patches")
        embedded = pair_sem("embedded")
        embedded_tok = pair_sem("embedded_tok")
        h_start = pair_sem("h_start")
        half_stats = pair_sem("half_stats")
        half_stats2 = pair_sem("half_stats2")
        moments = pair_sem("moments")
        eps_added = pair_sem("eps_added")
        rstd_ready = pair_sem("rstd_ready")
        normed = pair_sem("normed")
        turned = pair_sem("turned")
        yT_ready = pair_sem("yT_ready")
        scaled_tok = pair_sem("scaled_tok")
        qk_ready = pair_sem("qk_ready")
        v_ready = pair_sem("v_ready")
        rotated = pair_sem("rotated")
        hi_ready = pair_sem("hi_ready")
        v_padded = pair_sem("v_padded")
        lo_ready = pair_sem("lo_ready")
        rows_ready = [pair_sem(f"rows_ready_t{t}_") for t in range(2)]
        max_ready = [pair_sem(f"max_ready_t{t}_") for t in range(2)]
        max_turned = pair_sem("max_turned")
        max_in_q = pair_sem("max_in_q")
        scores_ready = [pair_sem(f"scores_ready_k{t}_") for t in range(2)]
        prob_ready = [pair_sem(f"prob_ready_k{t}_") for t in range(2)]
        masked = [pair_sem(f"masked_k{t}_") for t in range(2)]
        attended = pair_sem("attended")
        den_ready = pair_sem("den_ready")
        oT_ready = pair_sem("oT_ready")
        proj_ready = pair_sem("proj_ready")
        bias_added = pair_sem("bias_added")
        attn_added = pair_sem("attn_added")
        up_ready = pair_sem("up_ready")
        gelu_ready = pair_sem("gelu_ready")
        down_ready = pair_sem("down_ready")
        mlp_bias = pair_sem("mlp_bias")
        mlp_added = pair_sem("mlp_added")
        ret_qkv = pair_sem("ret_qkv")
        ret_q = pair_sem("ret_q")
        ret_kv = pair_sem("ret_kv")
        ret_scores = pair_sem("ret_scores")
        ret_weighted = pair_sem("ret_weighted")
        ret_read = pair_sem("ret_read")
        ret_turned = pair_sem("ret_turned")
        ret_out = pair_sem("ret_out")
        ret_added = pair_sem("ret_added")
        logits_ready = pair_sem("logits_ready")
        route = pair_sem("route")
        gap_ready = pair_sem("gap_ready")
        second_ready = pair_sem("second_ready")
        gates_ready = pair_sem("gates_ready")
        sum_ready = pair_sem("sum_ready")
        ex_up = pair_sem("ex_up")
        ex_gelu = pair_sem("ex_gelu")
        ex_down = pair_sem("ex_down")
        ex_added = pair_sem("ex_added")

        def carry(eng, k=0):
            if eng is nc.gpsimd:
                nc.gpsimd.tensor_tensor(carrier[:, k:k + 1], mhalf[:, 0:1], mhalf[:, 0:1], ALU.mult)
            else:
                nc.vector.memset(carrier[:, 4:5], 0.0)

        block = ctx.enter_context(nc.Block())

        @block.sync
        def _(sp):
            def load_images(pair):
                for s in SLOTS:
                    for c in range(3):
                        src = x[bass.ds(pair * 2 + s, 1), c, :, :].rearrange(
                            "o (gy py) w -> py (o gy) w", py=PATCH)
                        lo, hi = c * PATCH, (c + 1) * PATCH
                        sp.dma_start(img[s][lo:hi, :, :], src).then_inc(img_loaded[s], 16)
                        sp.dma_start(img[s][XSHIFT + lo:XSHIFT + hi, :, 0:IMG - HALF],
                                     src[:, :, HALF:IMG]).then_inc(img_loaded[s], 16)

            def load_expert(e, j):
                sp.dma_start(up_w[j][:, :], w1[bass.ds(e, 1), :, :].rearrange(
                    "o d f -> d (o f)")).then_inc(expert_loaded[j], 16)
                sp.dma_start(down_w[j][:, :, :], w2[bass.ds(e, 1), :, :].rearrange(
                    "o (c p) d -> p (o c) d", p=P)).then_inc(expert_loaded[j], 16)

            sp.wait_ge(pool_set, 1)
            load_images(0)
            sp.dma_start(cw[:, :], const_w[:, :]).then_inc(const_loaded, 16)
            sp.dma_start(aw[:, :], attn_w[0, :, :]).then_inc(attn_w_loaded, 16)
            sp.dma_start(mw[:, :], mlp_w[0, :, :]).then_inc(mlp_w_loaded, 16)
            for j in range(2):
                load_expert(j, j)
            with sp.Fori(0, PAIRS) as i:
                done = sp.snap(i + 1)
                for s in SLOTS:
                    sp.wait_ge(patches[s], done)
                load_images((i + 1) % PAIRS)
                with sp.Fori(0, LAYERS) as l:
                    layer_done = sp.snap(i * LAYERS + l + 1)
                    attn_done = sp.snap(i * ATTNS + l + 1)
                    coming = sp.snap((l + 1) % LAYERS)
                    for s in SLOTS:
                        sp.wait_ge(attn_added[s], attn_done)
                    sp.dma_start(aw[:, :], attn_w[bass.ds(coming, 1), :, :].rearrange(
                        "o p n -> p (o n)")).then_inc(attn_w_loaded, 16)
                    for s in SLOTS:
                        sp.wait_ge(mlp_added[s], layer_done)
                    sp.dma_start(mw[:, :], mlp_w[bass.ds(coming, 1), :, :].rearrange(
                        "o p n -> p (o n)")).then_inc(mlp_w_loaded, 16)
                with sp.Fori(0, EXPERTS // 2) as e:
                    for j in range(2):
                        expert_done = sp.snap(i * EXPERTS + e * 2 + j + 1)
                        for s in SLOTS:
                            sp.wait_ge(ex_down[s], expert_done)
                        load_expert(sp.snap((e * 2 + j + 2) % EXPERTS), j)
                for s in SLOTS:
                    sp.wait_ge(ex_added[s], sp.snap((i + 1) * EXPERTS))
                    for t, (t0, n) in enumerate(TILES):
                        sp.dma_start(out[bass.ds(i * 2 + s, 1), t0:t0 + n, :].rearrange(
                            "o t d -> t (o d)"), h[s][0:n, t, :]).then_inc(h_free[s], 16)
            for s in SLOTS:
                sp.wait_ge(h_free[s], 32 * (PAIRS + 1))
                sp.wait_ge(img_loaded[s], 96 * (PAIRS + 1))
            sp.wait_ge(attn_w_loaded, 16 * (PAIRS * LAYERS + 1))
            sp.wait_ge(mlp_w_loaded, 16 * (PAIRS * LAYERS + 1))
            for j in range(2):
                sp.wait_ge(expert_loaded[j], 32 * (PAIRS * EXPERTS // 2 + 1))

        @block.tensor
        def _(pe):
            mm = nc.tensor.matmul

            def turn(s, n):
                pe.wait_ge(normed[s], n)
                for t, (t0, m) in enumerate(TILES):
                    last = nc.tensor.transpose(bank(s, 3)[:, t0:t0 + m], yn[s][0:m, t, :], ident[0:m, 0:m])
                last.then_inc(turned[s], 1)

            def to_tokens(s, j, lhsT, w, sem_, start=True, stop=True):
                for t, (t0, m) in enumerate(TILES):
                    last = mm(bank(s, j)[0:m, t * D:(t + 1) * D], lhsT[:, t0:t0 + m], w, start=start, stop=stop)
                if sem_ is not None:
                    last.then_inc(sem_[s], 1)

            def project(s, j, w, col):
                for g in range(NGRP):
                    last = mm(bank(s, j)[:, g * NPAD:(g + 1) * NPAD], w[:, col + g * P:col + (g + 1) * P],
                              yT[s][:, :], start=True, stop=True)
                return last

            def strips(a):
                return [a[STRIP * r:STRIP * (r + 1)] for r in range(NSTRIP)]

            def row_scores(s, t, n, mask):
                t0, m = TILES[t]
                pe.wait_ge(hi_ready[s], n)
                if t == 0:
                    pe.wait_ge(lo_ready[s], n)
                    pe.wait_ge(v_padded[s], n)
                else:
                    pe.wait_ge(max_ready[0][s], n)
                if mask:
                    for r in range(NSTRIP):
                        for g in range(NGRP):
                            mm(bank(s, r)[0:m, g * NPAD:(g + 1) * NPAD], ident_r[:, 0:m],
                               causal_r[:, t, :], start=(g == 0), stop=False, skip_group_check=True)
                for g in range(NGRP):
                    for r in range(NSTRIP):
                        q = q_hi[s][STRIP * r:STRIP * (r + 1), g, t0:t0 + m]
                        k = k_hi[s][STRIP * r:STRIP * (r + 1), g, :]
                        last = mm(bank(s, r)[0:m, g * NPAD:(g + 1) * NPAD], q, k,
                                  start=not mask, stop=True, skip_group_check=mask)
                last.then_inc(rows_ready[t][s], 1)

            def place_max(s, n):
                pe.wait_ge(max_ready[1][s], n)
                for g in range(NGRP):
                    mm(bank(s, 0)[:, g * NPAD:g * NPAD + P], neg_max[s][:, 0, g, :], ident_r[:, 0:P],
                       start=True, stop=True)
                    m = TILES[1][1]
                    last = mm(bank(s, 0)[:, g * NPAD + P:(g + 1) * NPAD], neg_max[s][0:m, 1, g, :],
                              ident_r[0:m, 0:m + 1], start=True, stop=True)
                last.then_inc(max_turned[s], 1)

            def scores(s, t, n):
                t0, m = TILES[t]
                if t == 0:
                    pe.wait_ge(max_in_q[s], n)
                else:
                    pe.wait_ge(prob_ready[0][s], n)
                parts = ((k_hi, q_hi), (k_lo, q_hi), (k_hi, q_lo))
                for g in range(NGRP):
                    for c, (kk, qq) in enumerate(parts):
                        for r in range(NSTRIP):
                            last = mm(bank(s, r)[0:m, g * NPAD:(g + 1) * NPAD],
                                      kk[s][STRIP * r:STRIP * (r + 1), g, t0:t0 + m],
                                      qq[s][STRIP * r:STRIP * (r + 1), g, :],
                                      start=(c == 0), stop=(c == len(parts) - 1))
                last.then_inc(scores_ready[t][s], 1)

            def attend(s, ready, n):
                pe.wait_ge(prob_ready[1][s], n_attn[0])
                for t in range(2):
                    pe.wait_ge(ready[t][s], n)
                last_step = (1, NGRP - 1)
                for j in range(2):
                    for t, (t0, m) in enumerate(TILES):
                        for g in range(NGRP):
                            for r in range(NSTRIP):
                                w = vpad[s][0:m, t, r, g, :] if j == 0 else den_ones[0:m, g, :]
                                last = mm(bank(s, j)[STRIP * r:STRIP * (r + 1), 0:NTOK], w,
                                          prob[s][0:m, t, r, g * NPAD:g * NPAD + NTOK],
                                          start=((t, g) == (0, 0)), stop=((t, g) == last_step))
                last.then_inc(attended[s], 1)

            def out_project(s, w, n):
                pe.wait_ge(oT_ready[s], n)
                to_tokens(s, 2, oT[s], w, proj_ready)

            n_attn = [None]

            def after_projections(n, mask, ready, ready_n, w_out):
                n_attn[0] = n
                for t in range(2):
                    for s in SLOTS:
                        row_scores(s, t, n, mask)
                for s in SLOTS:
                    place_max(s, n)
                for t in range(2):
                    for s in SLOTS:
                        scores(s, t, n)
                for s in SLOTS:
                    attend(s, ready, ready_n)
                for s in SLOTS:
                    out_project(s, w_out, n)

            pe.wait_ge(const_loaded, 16)
            pe.wait_ge(pool_set, 2)
            pe.wait_ge(dve_set, 1)
            with pe.Fori(0, PAIRS) as i:
                pair = pe.snap(i + 1)
                img_n = pe.snap(i * 96 + 96)
                for s in SLOTS:
                    pe.wait_ge(img_loaded[s], img_n)
                    for px in range(HALF):
                        last = mm(bank(s, 0)[:, 0:NTOK - 1], cw[:, C_CONV + px * D:C_CONV + (px + 1) * D],
                                  img[s][:, :, px:IMG:PATCH], start=(px == 0), stop=(px == HALF - 1))
                    last.then_inc(patches[s], 1)
                for s in SLOTS:
                    pe.wait_ge(embedded[s], pair)
                    for t, (t0, m) in enumerate(TILES):
                        last = nc.tensor.transpose(bank(s, 1)[0:m, t * D:(t + 1) * D], oT[s][:, t0:t0 + m],
                                                   ident[:, :])
                    last.then_inc(embedded_tok[s], 1)
                with pe.Fori(0, LAYERS) as l:
                    layer = pe.snap(i * LAYERS + l + 1)
                    attn = pe.snap(i * ATTNS + l + 1)
                    norm = pe.snap(i * NORMS + l * 2 + 1)
                    yt = pe.snap(i * TURNS + l * 2 + 1)
                    norm2 = pe.snap(norm + 1)
                    yt2 = pe.snap(yt + 1)
                    w_n = pe.snap(layer * 16)
                    for s in SLOTS:
                        turn(s, norm)
                    pe.wait_ge(attn_w_loaded, w_n)
                    for s in SLOTS:
                        pe.wait_ge(yT_ready[s], yt)
                        project(s, 0, aw, A_WQ)
                        project(s, 1, aw, A_WK).then_inc(qk_ready[s], 1)
                        to_tokens(s, 2, yT[s], aw[:, A_WV:A_WV + D], v_ready)
                    after_projections(attn, False, prob_ready, attn, aw[:, A_WP:A_WP + D])
                    for s in SLOTS:
                        turn(s, norm2)
                    pe.wait_ge(mlp_w_loaded, w_n)
                    for s in SLOTS:
                        pe.wait_ge(yT_ready[s], yt2)
                        for c in range(HC):
                            last = mm(bank(s, 0)[:, c * NPAD:c * NPAD + NTOK],
                                      mw[:, M_W1 + c * P:M_W1 + (c + 1) * P], yT[s][:, 0:NTOK],
                                      start=True, stop=True)
                        last.then_inc(up_ready[s], 1)
                    for s in SLOTS:
                        pe.wait_ge(gelu_ready[s], layer)
                        for t, (t0, m) in enumerate(TILES):
                            for c in range(HC):
                                last = mm(bank(s, 1)[0:m, t * D:(t + 1) * D],
                                          gT[s][:, 0, c * NPAD + t0:c * NPAD + t0 + m],
                                          mw[:, M_W2 + c * D:M_W2 + (c + 1) * D],
                                          start=(c == 0), stop=(c == HC - 1))
                        last.then_inc(down_ready[s], 1)
                norm = pe.snap(i * NORMS + 2 * LAYERS + 2)
                yt = pe.snap(i * TURNS + 2 * LAYERS + 1)
                for s in SLOTS:
                    turn(s, norm)
                for s in SLOTS:
                    pe.wait_ge(yT_ready[s], yt)
                    mm(bank(s, 0)[:, 0:NTOK], cw[:, C_RQ:C_RQ + D], yT[s][:, 0:NTOK], start=True, stop=True)
                    mm(bank(s, 1)[:, 0:NTOK], cw[:, C_RK:C_RK + D], yT[s][:, 0:NTOK], start=True, stop=True)
                    to_tokens(s, 2, yT[s], cw[:, C_RV:C_RV + D], ret_qkv)
                for s in SLOTS:
                    pe.wait_ge(ret_q[s], pair)
                    pe.wait_ge(ret_kv[s], pair)
                    for t, (t0, m) in enumerate(TILES):
                        last = mm(bank(s, t)[0:m, 0:NTOK], k_rot[s][:, t0:t0 + m], q_rot[s][:, 0:NTOK],
                                  start=True, stop=True)
                    last.then_inc(ret_scores[s], 1)
                for s in SLOTS:
                    pe.wait_ge(ret_weighted[s], pair)
                    for t, (t0, m) in enumerate(TILES):
                        last = mm(bank(s, 2)[:, 0:NTOK], rkv[s][0:m, t, :], rot[s][0:m, t, 0:NTOK],
                                  start=(t == 0), stop=(t == 1))
                    last.then_inc(ret_read[s], 1)
                for s in SLOTS:
                    pe.wait_ge(ret_turned[s], pair)
                    to_tokens(s, 3, oT[s], cw[:, C_RO:C_RO + D], ret_out)
                norm = pe.snap(norm + 2)
                yt = pe.snap(yt + 1)
                attn = pe.snap(i * ATTNS + ATTNS)
                for s in SLOTS:
                    turn(s, norm)
                for s in SLOTS:
                    pe.wait_ge(yT_ready[s], yt)
                    for j, col in enumerate((C_FWQ, C_FWQS, C_FWK, C_FWKS)):
                        last = project(s, j, cw, col)
                    last.then_inc(qk_ready[s], 1)
                for s in SLOTS:
                    pe.wait_ge(rotated[s], pe.snap(i * 6 + 6))
                    to_tokens(s, 2, yT[s], cw[:, C_FWV:C_FWV + D], v_ready)
                after_projections(attn, True, masked, pair, cw[:, C_FWO:C_FWO + D])
                norm = pe.snap(norm + 1)
                yt = pe.snap(yt + 1)
                for s in SLOTS:
                    turn(s, norm)
                for s in SLOTS:
                    pe.wait_ge(yT_ready[s], yt)
                    for t, (t0, m) in enumerate(TILES):
                        last = mm(bank(s, 2)[0:m, t * EXPERTS:(t + 1) * EXPERTS], yT[s][:, t0:t0 + m],
                                  cw[:, C_ROUT:C_ROUT + EXPERTS], start=True, stop=True)
                    last.then_inc(logits_ready[s], 1)
                with pe.Fori(0, EXPERTS // 2) as e:
                    for s in SLOTS:
                        pe.wait_ge(gates_ready[s], pair)
                    load_n = pe.snap((i * (EXPERTS // 2) + e + 1) * 32)
                    for j in range(2):
                        expert = pe.snap(i * EXPERTS + e * 2 + j + 1)
                        pe.wait_ge(expert_loaded[j], load_n)
                        for s in SLOTS:
                            for c in range(FC):
                                last = mm(bank(s, c // 2)[:, c % 2 * NPAD:c % 2 * NPAD + NTOK],
                                          up_w[j][:, c * P:(c + 1) * P], yT[s][:, 0:NTOK],
                                          start=True, stop=True)
                            last.then_inc(ex_up[s], 1)
                        for s in SLOTS:
                            pe.wait_ge(ex_gelu[s], expert)
                            for t, (t0, m) in enumerate(TILES):
                                for c in range(FC):
                                    last = mm(bank(s, 2 + j)[0:m, t * D:(t + 1) * D],
                                              gT[s][:, c // 2, c % 2 * NPAD + t0:c % 2 * NPAD + t0 + m],
                                              down_w[j][:, c, :], start=(c == 0), stop=(c == FC - 1))
                            last.then_inc(ex_down[s], 1)
                    for s in SLOTS:
                        pe.wait_ge(ex_added[s], expert)

        @block.scalar
        def _(act):
            run = nc.scalar.activation

            def col(w, c):
                return w[:, c:c + 1]

            def to_yT(s, n, scale=None, bias=None):
                act.wait_ge(turned[s], n)
                kw = {"scale": scale} if scale is not None else {}
                if bias is not None:
                    kw["bias"] = bias
                run(yT[s][:, 0:NTOK], bank(s, 3)[:, 0:NTOK],
                    ACT.Copy if not kw else ACT.Identity, **kw).then_inc(yT_ready[s], 1)

            def hi(s, q_src, k_src, q_bias, k_bias):
                for g in range(NGRP):
                    run(q_hi[s][:, g, :], q_src[:, g * NPAD:(g + 1) * NPAD], ACT.Identity, bias=q_bias[g])
                for g in range(NGRP):
                    last = run(k_hi[s][:, g, :], k_src[:, g * NPAD:(g + 1) * NPAD], ACT.Identity,
                               bias=k_bias[g])
                last.then_inc(hi_ready[s], 1)

            def exps(s, t, n):
                m = TILES[t][1]
                act.wait_ge(scores_ready[t][s], n)
                run(prob[s][0:m, t, :, :], psum[0:m, 4 * s:4 * s + NSTRIP, 0:GW], ACT.Exp,
                    scale=SCALE).then_inc(prob_ready[t][s], 1)

            act.wait_ge(dve_set, 3)
            run(lnd[:, 2:3], lnd[:, 1:2], ACT.Exp).then_inc(act_set, 1)
            act.wait_ge(act_set, 1)
            run(lnd[:, 3:4], lnd[:, 2:3], ACT.Ln, bias=1.0).then_inc(act_set, 1)
            act.wait_ge(dve_set, 5)
            run(decay_t[:, :, :], causal[:, :, :], ACT.Exp, scale=lnd[:, 5:6]).then_inc(act_set, 1)
            with act.Fori(0, PAIRS) as i:
                pair = act.snap(i + 1)
                with act.Fori(0, LAYERS) as l:
                    layer = act.snap(i * LAYERS + l + 1)
                    attn = act.snap(i * ATTNS + l + 1)
                    yt = act.snap(i * TURNS + l * 2 + 1)
                    yt2 = act.snap(yt + 1)
                    w_n = act.snap(layer * 16)
                    act.wait_ge(attn_w_loaded, w_n)
                    for s in SLOTS:
                        to_yT(s, yt, col(aw, A_COL), col(aw, A_COL + 1))
                    for s in SLOTS:
                        act.wait_ge(qk_ready[s], attn)
                        hi(s, bank(s, 0), bank(s, 1), [col(aw, A_COL + 2), col(aw, A_COL + 3)],
                           [col(aw, A_COL + 4), col(aw, A_COL + 5)])
                    for t in range(2):
                        for s in SLOTS:
                            exps(s, t, attn)
                    act.wait_ge(mlp_w_loaded, w_n)
                    for s in SLOTS:
                        to_yT(s, yt2, col(mw, M_COL), col(mw, M_COL + 1))
                    for s in SLOTS:
                        act.wait_ge(up_ready[s], layer)
                        for c in range(HC):
                            last = run(gT[s][:, 0, c * NPAD:c * NPAD + NTOK],
                                       bank(s, 0)[:, c * NPAD:c * NPAD + NTOK], ACT.Gelu,
                                       bias=col(mw, M_COL + 2 + c))
                        last.then_inc(gelu_ready[s], 1)
                yt = act.snap(i * TURNS + 2 * LAYERS + 1)
                for s in SLOTS:
                    to_yT(s, yt)
                for s in SLOTS:
                    act.wait_ge(ret_qkv[s], pair)
                    run(q_rot[s][:, 0:NTOK], bank(s, 0)[:, 0:NTOK], ACT.Copy).then_inc(ret_q[s], 1)
                for s in SLOTS:
                    act.wait_ge(ret_read[s], pair)
                    run(oT[s][:, :], bank(s, 2)[:, 0:NTOK], ACT.Copy).then_inc(ret_turned[s], 1)
                yt = act.snap(yt + 1)
                attn = act.snap(i * ATTNS + ATTNS)
                rot_n = act.snap(i * 6 + 6)
                for s in SLOTS:
                    to_yT(s, yt, col(cw, C_FW1))
                for s in SLOTS:
                    act.wait_ge(rotated[s], rot_n)
                    hi(s, q_rot[s], k_rot[s], [col(cw, C_ZERO)] * 2, [col(cw, C_ONE)] * 2)
                for t in range(2):
                    for s in SLOTS:
                        exps(s, t, attn)
                yt = act.snap(yt + 1)
                for s in SLOTS:
                    to_yT(s, yt, col(cw, C_FW2))
                for s in SLOTS:
                    act.wait_ge(gap_ready[s], pair)
                    run(second[s][:, :], gap[s][:, :], ACT.Exp).then_inc(second_ready[s], 1)
                with act.Fori(0, EXPERTS) as e:
                    expert = act.snap(i * EXPERTS + e + 1)
                    for s in SLOTS:
                        act.wait_ge(ex_up[s], expert)
                        run(gT[s][:, :, :].rearrange("p a (c n) -> p a c n", c=2)[:, :, :, 0:NTOK],
                            psum[:, 4 * s:4 * s + 2, 0:GW].rearrange("p a (c n) -> p a c n", c=2)[:, :, :, 0:NTOK],
                            ACT.Gelu).then_inc(ex_gelu[s], 1)

        @block.gpsimd
        def _(pool):
            for s in SLOTS:
                last = nc.gpsimd.memset(img[s][:, :, :], 0.0)
            last.then_inc(pool_set, 1)
            for s in SLOTS:
                for a in (hh, yn, yT, stats, mv, ve, gap, gates, logit, den, second, vpad, topf, gate, top, rstd):
                    nc.gpsimd.memset(a[s][:], 0.0)
                nc.gpsimd.memset(h[s][:, :, :], 0.0).then_inc(h_free[s], 32)
            nc.gpsimd.memset(mhalf[:, :], -0.5)
            nc.gpsimd.memset(eps2[:, :], EPS)
            nc.gpsimd.memset(den_ones[:, :, :], 0.0)
            nc.gpsimd.memset(causal[:, :, :], 0.0)
            nc.gpsimd.iota(expert_i[:, :], pattern=[[1, EXPERTS]], base=0, channel_multiplier=0)
            nc.gpsimd.memset(ident[:, :], 0.0).then_inc(pool_set, 1)
            pool.wait_ge(pool_set, 2)
            for g in range(NGRP):
                nc.gpsimd.memset(den_ones[:, g, g * HD:(g + 1) * HD], 1.0)
            for t, (t0, _) in enumerate(TILES):
                nc.gpsimd.iota(expo_i[:, t, :], pattern=[[-1, NPAD]], base=t0 - 1, channel_multiplier=1)
                nc.gpsimd.affine_select(out=causal[:, t, :], in_=causal[:, t, :], pattern=[[-1, NPAD]],
                                        compare_op=ALU.is_ge, fill=MASKED, base=t0, channel_multiplier=1)
            nc.gpsimd.affine_select(out=ident[:, :], in_=ident[:, :], pattern=[[-1, P]],
                                    compare_op=ALU.not_equal, fill=1.0, base=0,
                                    channel_multiplier=1).then_inc(pool_set, 1)
            pool.wait_ge(act_set, 3)
            for t, (t0, _) in enumerate(TILES):
                last = nc.gpsimd.affine_select(out=decay_t[:, t, :], in_=decay_t[:, t, :], pattern=[[-1, NPAD]],
                                               compare_op=ALU.is_gt, fill=0.0, base=t0, channel_multiplier=1)
            last.then_inc(pool_set, 1)

            def invert(s, n):
                pool.wait_ge(moments[s], n)
                nc.gpsimd.tensor_tensor(ve[s][:, :], ve[s][:, :], eps2[:, :], ALU.add).then_inc(eps_added[s], 1)
                pool.wait_ge(eps_added[s], n)
                nc.gpsimd.tensor_tensor(rstd[s][:, :], ve[s][:, :], mhalf[:, :], ALU.pow).then_inc(rstd_ready[s], 1)

            def add_rows(s, dst, src, sem_):
                for t, (_, m) in enumerate(TILES):
                    last = nc.gpsimd.tensor_tensor(dst[s][0:m, t, :], dst[s][0:m, t, :],
                                                   src[0:m, :] if src is not None else hh[s][0:m, t, :], ALU.add)
                last.then_inc(sem_[s], 1)

            with pool.Fori(0, PAIRS) as i:
                pair = pool.snap(i + 1)
                with pool.Fori(0, LAYERS) as l:
                    layer = pool.snap(i * LAYERS + l + 1)
                    norm = pool.snap(i * NORMS + l * 2 + 1)
                    norm2 = pool.snap(norm + 1)
                    w_n = pool.snap(layer * 16)
                    for s in SLOTS:
                        invert(s, norm)
                    pool.wait_ge(attn_w_loaded, w_n)
                    for s in SLOTS:
                        pool.wait_ge(normed[s], norm)
                        add_rows(s, h, aw[:, A_BP:A_BP + D], bias_added)
                    for s in SLOTS:
                        invert(s, norm2)
                    pool.wait_ge(mlp_w_loaded, w_n)
                    for s in SLOTS:
                        pool.wait_ge(normed[s], norm2)
                        add_rows(s, h, mw[:, M_B2:M_B2 + D], mlp_bias)
                for j in range(4):
                    norm = pool.snap(i * NORMS + 2 * LAYERS + 1 + j)
                    for s in SLOTS:
                        invert(s, norm)
                attn = pool.snap(i * ATTNS + ATTNS)
                for t, (t0, m) in enumerate(TILES):
                    for s in SLOTS:
                        pool.wait_ge(prob_ready[t][s], attn)
                        carry(nc.gpsimd, 2 * t + s)
                        p = prob[s][0:m, t, :, :].rearrange("p r (g n) -> p (r g) n", g=NGRP)
                        nc.gpsimd.affine_select(out=p, in_=p, pattern=[[0, HEADS], [1, NPAD]],
                                                compare_op=ALU.is_ge, fill=0.0, base=-t0,
                                                channel_multiplier=-1).then_inc(masked[t][s], 1)
                norm = pool.snap(i * NORMS + NORMS)
                for s in SLOTS:
                    invert(s, norm)
                for s in SLOTS:
                    pool.wait_ge(normed[s], norm)
                    add_rows(s, h, None, sum_ready)

        @block.vector
        def _(dve):
            v = nc.vector

            def moments_of(s, src, n, rms=False):
                for t, (_, m) in enumerate(TILES):
                    last = v.bn_stats(stats[s][0:m, t, :], src[s][0:m, t, :])
                last.then_inc(half_stats[s], 1)
                dve.wait_ge(half_stats[s], n)
                carry(nc.vector)
                for t, (_, m) in enumerate(TILES):
                    last = v.bn_aggr(mv[s][0:m, t, :], stats[s][0:m, t, :])
                last.then_inc(half_stats2[s], 1)
                dve.wait_ge(half_stats2[s], n)
                if rms:
                    for t, (_, m) in enumerate(TILES):
                        last = v.scalar_tensor_tensor(ve[s][0:m, t:t + 1], mv[s][0:m, t, 0:1], mv[s][0:m, t, 0:1],
                                                      mv[s][0:m, t, 1:2], ALU.mult, ALU.add)
                else:
                    last = v.tensor_copy(ve[s][:, :], mv[s][:, :, 1])
                last.then_inc(moments[s], 1)

            def apply(s, src, dst, n, rms=False):
                dve.wait_ge(rstd_ready[s], n)
                for t, (_, m) in enumerate(TILES):
                    if rms:
                        last = v.tensor_scalar(dst[s][0:m, t, :], src[s][0:m, t, :], rstd[s][0:m, t:t + 1], None,
                                               ALU.mult)
                    else:
                        last = v.tensor_scalar(dst[s][0:m, t, :], src[s][0:m, t, :], mv[s][0:m, t, 0:1],
                                               rstd[s][0:m, t:t + 1], ALU.subtract, ALU.mult)
                last.then_inc(normed[s], 1)

            def lo(s, q_src, k_src, q_bias, k_bias, n):
                dve.wait_ge(hi_ready[s], n)
                for g in range(NGRP):
                    sl = slice(g * NPAD, (g + 1) * NPAD)
                    v.scalar_tensor_tensor(q_lo[s][:, g, :], q_src[:, sl], q_bias[g],
                                           q_hi[s][:, g, :].bitcast(F32), ALU.add, ALU.subtract)
                    last = v.scalar_tensor_tensor(k_lo[s][:, g, :], k_src[:, sl], k_bias[g],
                                                  k_hi[s][:, g, :].bitcast(F32), ALU.add, ALU.subtract)
                last.then_inc(lo_ready[s], 1)

            def pad_v(s, bias, n):
                dve.wait_ge(v_ready[s], n)
                for t, (_, m) in enumerate(TILES):
                    src = bank(s, 2)[0:m, t * D:(t + 1) * D].rearrange("p (r g d) -> p g r d", g=NGRP, d=HD)
                    for g in range(NGRP):
                        dst = vpad[s][0:m, t, :, g, g * HD:(g + 1) * HD]
                        if bias is None:
                            last = v.tensor_copy(dst, src[:, g])
                        else:
                            b = bias[0:m, :].rearrange("p (r g d) -> p g r d", g=NGRP, d=HD)
                            last = v.tensor_tensor(dst, src[:, g], b[:, g], ALU.add)
                last.then_inc(v_padded[s], 1)

            def maxima(s, t, n):
                m = TILES[t][1]
                dve.wait_ge(rows_ready[t][s], n)
                src = psum[0:m, 4 * s:4 * s + NSTRIP, 0:GW].rearrange("p r (g n) -> p r g n", g=NGRP)
                dst = neg_max[s][0:m, t, :, :].rearrange("p g (r c) -> p r g c", c=STRIP)[:, :, :, HD:HD + 1]
                v.tensor_reduce(dst, src[:, :, :, 0:NTOK], AX, ALU.max, negate=True).then_inc(max_ready[t][s], 1)

            def put_max(s, n):
                dve.wait_ge(max_turned[s], n)
                q = q_hi[s][:, :, :].rearrange("p g n -> p (g n)")
                v.tensor_tensor(q, bank(s, 0)[:, 0:GW], q.bitcast(F32), ALU.add).then_inc(max_in_q[s], 1)

            def normalise(s, n):
                dve.wait_ge(attended[s], n)
                v.reciprocal(rden[s][:, :], bank(s, 1)[:, 0:NTOK]).then_inc(den_ready[s], 1)
                dve.wait_ge(den_ready[s], n)
                v.tensor_tensor(oT[s][:, :], bank(s, 0)[:, 0:NTOK], rden[s][:, :], ALU.mult).then_inc(oT_ready[s], 1)

            def add_tokens(s, dst, j, sem_):
                for t, (_, m) in enumerate(TILES):
                    last = v.tensor_tensor(dst[s][0:m, t, :], bank(s, j)[0:m, t * D:(t + 1) * D], dst[s][0:m, t, :],
                                           ALU.add)
                last.then_inc(sem_[s], 1)

            def attention(n):
                for t in range(2):
                    for s in SLOTS:
                        maxima(s, t, n)
                for s in SLOTS:
                    put_max(s, n)
                for s in SLOTS:
                    normalise(s, n)

            dve.wait_ge(pool_set, 3)
            v.tensor_copy(ident_r[:, :], ident[:, :])
            v.tensor_copy(causal_r[:, :, :], causal[:, :, :])
            v.tensor_copy(expert_f[:, :], expert_i[:, :])
            for s in SLOTS:
                last = v.memset(neg_max[s][:, :, :, :].bitcast(U32), 0)
            last.then_inc(dve_set, 1)
            dve.wait_ge(const_loaded, 16)
            v.tensor_scalar(posT[:, 1:NTOK], cw[:, C_POS + 1:C_POS + NTOK], cw[:, C_CONVB:C_CONVB + 1], None, ALU.add)
            v.tensor_scalar(posT[:, 0:1], cw[:, C_POS:C_POS + 1], cw[:, C_CLS:C_CLS + 1], None, ALU.add)
            v.tensor_scalar(lnd[:, 0:1], cw[:, C_DECAY:C_DECAY + 1], -1.0, None, ALU.mult).then_inc(dve_set, 1)
            dve.wait_ge(dve_set, 2)
            v.tensor_scalar(lnd[:, 4:5], lnd[:, 0:1], 0.0, None, ALU.max)
            v.tensor_tensor(lnd[:, 1:2], lnd[:, 0:1], cw[:, C_DECAY:C_DECAY + 1], ALU.min).then_inc(dve_set, 1)
            dve.wait_ge(act_set, 2)
            v.scalar_tensor_tensor(lnd[:, 5:6], lnd[:, 3:4], -1.0, lnd[:, 4:5], ALU.mult,
                                   ALU.subtract).then_inc(dve_set, 1)
            v.tensor_scalar(causal[:, :, :], expo_i[:, :, :], 0.0, None, ALU.max).then_inc(dve_set, 1)
            dve.wait_ge(pool_set, 4)
            with dve.Fori(0, PAIRS) as i:
                pair = dve.snap(i + 1)
                free_n = dve.snap(i * 32 + 32)
                for s in SLOTS:
                    dve.wait_ge(patches[s], pair)
                    v.tensor_copy(oT[s][:, 0:1], posT[:, 0:1])
                    v.tensor_tensor(oT[s][:, 1:NTOK], bank(s, 0)[:, 0:NTOK - 1], posT[:, 1:NTOK],
                                    ALU.add).then_inc(embedded[s], 1)
                for s in SLOTS:
                    dve.wait_ge(embedded_tok[s], pair)
                    dve.wait_ge(h_free[s], free_n)
                    for t, (_, m) in enumerate(TILES):
                        last = v.tensor_copy(h[s][0:m, t, :], bank(s, 1)[0:m, t * D:(t + 1) * D])
                    last.then_inc(h_start[s], 1)
                with dve.Fori(0, LAYERS) as l:
                    for s in SLOTS:
                        dve.wait_ge(h_start[s], pair)
                    layer = dve.snap(i * LAYERS + l + 1)
                    attn = dve.snap(i * ATTNS + l + 1)
                    norm = dve.snap(i * NORMS + l * 2 + 1)
                    norm2 = dve.snap(norm + 1)
                    w_n = dve.snap(layer * 16)
                    for s in SLOTS:
                        moments_of(s, h, norm)
                    for s in SLOTS:
                        apply(s, h, yn, norm)
                    dve.wait_ge(attn_w_loaded, w_n)
                    for s in SLOTS:
                        pad_v(s, aw[:, A_BV:A_BV + D], attn)
                        lo(s, bank(s, 0), bank(s, 1), [aw[:, A_COL + 2 + g:A_COL + 3 + g] for g in range(NGRP)],
                           [aw[:, A_COL + 4 + g:A_COL + 5 + g] for g in range(NGRP)], attn)
                    attention(attn)
                    for s in SLOTS:
                        dve.wait_ge(bias_added[s], layer)
                        dve.wait_ge(proj_ready[s], attn)
                        add_tokens(s, h, 2, attn_added)
                    for s in SLOTS:
                        dve.wait_ge(attn_added[s], attn)
                        moments_of(s, h, norm2)
                    for s in SLOTS:
                        apply(s, h, yn, norm2)
                    for s in SLOTS:
                        dve.wait_ge(mlp_bias[s], layer)
                        dve.wait_ge(down_ready[s], layer)
                        add_tokens(s, h, 1, mlp_added)
                    for s in SLOTS:
                        dve.wait_ge(mlp_added[s], layer)
                norm = dve.snap(i * NORMS + 2 * LAYERS + 1)
                tok_n = dve.snap(i * 2 + 1)
                for s in SLOTS:
                    moments_of(s, h, norm)
                for s in SLOTS:
                    apply(s, h, yn, norm)
                for s in SLOTS:
                    dve.wait_ge(normed[s], norm)
                    for t, (_, m) in enumerate(TILES):
                        last = v.tensor_tensor(h[s][0:m, t, :], yn[s][0:m, t, :], cw[0:m, C_NW:C_NW + D], ALU.mult)
                    last.then_inc(scaled_tok[s], 1)
                for s in SLOTS:
                    dve.wait_ge(scaled_tok[s], tok_n)
                    for t, (_, m) in enumerate(TILES):
                        last = v.tensor_tensor(h[s][0:m, t, :], h[s][0:m, t, :], cw[0:m, C_NB:C_NB + D], ALU.add)
                    last.then_inc(scaled_tok[s], 1)
                norm = dve.snap(norm + 1)
                tok_n = dve.snap(tok_n + 1)
                for s in SLOTS:
                    dve.wait_ge(scaled_tok[s], tok_n)
                    moments_of(s, h, norm)
                for s in SLOTS:
                    apply(s, h, yn, norm)
                for s in SLOTS:
                    dve.wait_ge(ret_qkv[s], pair)
                    v.tensor_copy(k_rot[s][:, 0:NTOK], bank(s, 1)[:, 0:NTOK])
                    for t, (_, m) in enumerate(TILES):
                        last = v.tensor_copy(rkv[s][0:m, t, :], bank(s, 2)[0:m, t * D:(t + 1) * D])
                    last.then_inc(ret_kv[s], 1)
                for s in SLOTS:
                    dve.wait_ge(ret_scores[s], pair)
                    for t, (_, m) in enumerate(TILES):
                        last = v.tensor_tensor(rot[s][0:m, t, 0:NTOK], bank(s, t)[0:m, 0:NTOK],
                                               decay_t[0:m, t, 0:NTOK], ALU.mult)
                    last.then_inc(ret_weighted[s], 1)
                for s in SLOTS:
                    dve.wait_ge(ret_out[s], pair)
                    for t, (_, m) in enumerate(TILES):
                        last = v.scalar_tensor_tensor(h[s][0:m, t, :], bank(s, 3)[0:m, t * D:(t + 1) * D],
                                                      cw[0:m, C_SCALE:C_SCALE + 1], h[s][0:m, t, :],
                                                      ALU.mult, ALU.add)
                    last.then_inc(ret_added[s], 1)
                norm = dve.snap(norm + 1)
                for s in SLOTS:
                    dve.wait_ge(ret_added[s], pair)
                    moments_of(s, h, norm)
                for s in SLOTS:
                    apply(s, h, hh, norm)
                norm2 = dve.snap(norm + 1)
                for s in SLOTS:
                    dve.wait_ge(normed[s], norm)
                    moments_of(s, hh, norm2, rms=True)
                for s in SLOTS:
                    apply(s, hh, yn, norm2, rms=True)
                attn = dve.snap(i * ATTNS + ATTNS)
                step = dve.snap(i * 6)
                for s in SLOTS:
                    dve.wait_ge(qk_ready[s], attn)
                    cos, sin = cw[:, C_COS:C_COS + GW], cw[:, C_SIN:C_SIN + GW]
                    for j, dst in enumerate((q_rot, k_rot)):
                        v.tensor_tensor(dst[s][:, :], bank(s, 2 * j)[:, 0:GW], cos, ALU.mult).then_inc(rotated[s], 1)
                        v.tensor_tensor(rot[s][:, j, :], bank(s, 2 * j + 1)[:, 0:GW], sin,
                                        ALU.mult).then_inc(rotated[s], 1)
                    dve.wait_ge(rotated[s], step + 4)
                    for j, dst in enumerate((q_rot, k_rot)):
                        v.tensor_tensor(dst[s][:, :], dst[s][:, :], rot[s][:, j, :], ALU.add).then_inc(rotated[s], 1)
                for s in SLOTS:
                    pad_v(s, None, attn)
                    lo(s, q_rot[s], k_rot[s], [cw[:, C_ZERO:C_ZERO + 1]] * 2, [cw[:, C_ONE:C_ONE + 1]] * 2, attn)
                attention(attn)
                for s in SLOTS:
                    dve.wait_ge(proj_ready[s], attn)
                    add_tokens(s, hh, 2, attn_added)
                norm = dve.snap(i * NORMS + NORMS)
                for s in SLOTS:
                    dve.wait_ge(attn_added[s], attn)
                    moments_of(s, hh, norm, rms=True)
                for s in SLOTS:
                    apply(s, hh, yn, norm, rms=True)
                r0 = dve.snap(i * 9)
                for s in SLOTS:
                    def link(k, ins, s=s):
                        ins.then_inc(route[s], 1)
                        dve.wait_ge(route[s], r0 + k)

                    dve.wait_ge(logits_ready[s], pair)
                    for t, (_, m) in enumerate(TILES):
                        last = v.tensor_copy(logit[s][0:m, t, :], bank(s, 2)[0:m, t * EXPERTS:(t + 1) * EXPERTS])
                    link(1, last)
                    carry(nc.vector)
                    for t in range(2):
                        last = v.max(top[s][:, t, :], logit[s][:, t, :])
                    link(2, last)
                    v.tensor_tensor(gap[s][:, :], top[s][:, :, 1], top[s][:, :, 0],
                                    ALU.subtract).then_inc(gap_ready[s], 1)
                    for t in range(2):
                        last = v.max_index(topi[s][:, t, :], top[s][:, t, :], logit[s][:, t, :])
                    link(3, last)
                    link(4, v.tensor_copy(topf[s][:, :, :], topi[s][:, :, 0:2]))
                    dve.wait_ge(second_ready[s], pair)
                    link(5, v.tensor_scalar(den[s][:, :], second[s][:, :], 1.0, None, ALU.add))
                    link(6, v.reciprocal(gate[s][:, :, 0], den[s][:, :]))
                    link(7, v.tensor_tensor(gate[s][:, :, 1], gate[s][:, :, 0], second[s][:, :], ALU.mult))
                    for t in range(2):
                        v.tensor_scalar(gates2[s][:, t, :], expert_f[:, :], topf[s][:, t, 1:2],
                                        gate[s][:, t, 1:2], ALU.is_equal, ALU.mult)
                    for t in range(2):
                        last = v.tensor_scalar(gates[s][:, t, :], expert_f[:, :], topf[s][:, t, 0:1],
                                               gate[s][:, t, 0:1], ALU.is_equal, ALU.mult)
                    link(8, last)
                    link(9, v.tensor_tensor(gates[s][:, :, :], gates[s][:, :, :], gates2[s][:, :, :], ALU.add))
                    dve.wait_ge(sum_ready[s], pair)
                    v.tensor_copy(gate[s][:, :, :], topf[s][:, :, :]).then_inc(gates_ready[s], 1)
                with dve.Fori(0, EXPERTS // 2) as e:
                    for j in range(2):
                        expert = dve.snap(i * EXPERTS + e * 2 + j + 1)
                        for s in SLOTS:
                            dve.wait_ge(ex_down[s], expert)
                            for t, (_, m) in enumerate(TILES):
                                g = gates[s][0:m, t, bass.ds(e * 2 + j, 1)]
                                last = v.scalar_tensor_tensor(h[s][0:m, t, :], bank(s, 2 + j)[0:m, t * D:(t + 1) * D],
                                                              g, h[s][0:m, t, :], ALU.mult, ALU.add)
                            last.then_inc(ex_added[s], 1)
                        for s in SLOTS:
                            dve.wait_ge(ex_added[s], expert)


def columns(*parts):
    return np.ascontiguousarray(np.concatenate([np.asarray(p, np.float32).reshape(P, -1) for p in parts], axis=1))


def heads_to_strips(w):
    w = np.asarray(w, np.float32)
    out = np.zeros((w.shape[0], NGRP, NSTRIP, STRIP), np.float32)
    out[..., :HD] = w.reshape(w.shape[0], NSTRIP, NGRP, HD).transpose(0, 2, 1, 3)
    return out.reshape(w.shape[0], NGRP * P)


def swapped(w):
    return np.asarray(w).reshape(D, D // 2, 2)[:, :, ::-1].reshape(D, D)


def rope_tables():
    inv = (1.0 / np.float32(10000.0) ** (np.arange(0, HD, 2, dtype=np.float32) / np.float32(HD))).astype(np.float32)
    ang = np.arange(NPAD, dtype=np.float32)[:, None] * inv[None, :]
    cos, sin = np.zeros((STRIP, NPAD), np.float32), np.zeros((STRIP, NPAD), np.float32)
    cos[0:HD:2], cos[1:HD:2] = np.cos(ang).T, np.cos(ang).T
    sin[0:HD:2], sin[1:HD:2] = -np.sin(ang).T, np.sin(ang).T
    return [np.tile(np.tile(a, (NSTRIP, 1)), (1, NGRP)) for a in (cos, sin)]


def one_row():
    a = np.zeros((P, 1), np.float32)
    a[HD::STRIP] = 1.0
    return a


def kernel(**inputs):
    import concourse.bacc as bacc
    from concourse.bass_utils import run_bass_kernel_spmd

    a = {k: np.asarray(v) for k, v in inputs.items()}

    def rows(v):
        return np.broadcast_to(np.asarray(v).reshape(1, -1), (P, np.asarray(v).size))

    attn_w, mlp_w = [], []
    for l in range(LAYERS):
        w, b = a["L0_tok_qkv_w"][l], a["L0_tok_qkv_b"][l].reshape(1, -1)
        q_bias = heads_to_strips(b[:, 0:D]).reshape(NGRP, P).T
        k_bias = heads_to_strips(b[:, D:2 * D]).reshape(NGRP, P).T.copy()
        k_bias[HD::STRIP] = 1.0
        attn_w.append(columns(heads_to_strips(w[:, 0:D]), heads_to_strips(w[:, D:2 * D]), w[:, 2 * D:3 * D],
                              a["L0_tok_proj_w"][l], rows(b[:, 2 * D:3 * D]), rows(a["L0_tok_proj_b"][l]),
                              a["L0_tok_ln1_w"][l], a["L0_tok_ln1_b"][l], q_bias, k_bias))
        mlp_w.append(columns(a["L0_tok_fc1_w"][l], a["L0_tok_fc2_w"][l].reshape(HC, P, D).transpose(1, 0, 2),
                             rows(a["L0_tok_fc2_b"][l]), a["L0_tok_ln2_w"][l], a["L0_tok_ln2_b"][l],
                             a["L0_tok_fc1_b"][l].reshape(HC, P).T))
    conv = np.zeros((P, HALF, D), np.float32)
    cv = a["L0_tok_conv_w"].reshape(XROWS, PATCH, D)
    conv[0:XROWS] = cv[:, 0:HALF]
    conv[XSHIFT:XSHIFT + XROWS] = cv[:, HALF:PATCH]
    cos, sin = rope_tables()
    const_w = columns(
        conv, heads_to_strips(a["L0_ffn_wq"]), heads_to_strips(swapped(a["L0_ffn_wq"])),
        heads_to_strips(a["L0_ffn_wk"]), heads_to_strips(swapped(a["L0_ffn_wk"])), a["L0_ffn_wv"], a["L0_ffn_wo"],
        a["L0_attn_Wq"].T, a["L0_attn_Wk"].T, a["L0_attn_Wv"].T, a["L0_attn_Wo"].T, a["L0_ffn_router_w"],
        rows(a["L0_tok_norm_w"]), rows(a["L0_tok_norm_b"]), a["L0_tok_pos_embed"][0].T, cos, sin, one_row(),
        np.zeros((P, 1), np.float32), a["L0_ffn_attn_norm_w"], a["L0_ffn_ffn_norm_w"], a["L0_tok_conv_b"],
        a["L0_tok_cls_token"], rows(a["L0_attn_decay_logit"]), rows(a["L0_attn_out_scale"]))
    assert const_w.shape[1] == C_N and attn_w[0].shape[1] == A_N and mlp_w[0].shape[1] == M_N
    arrays = {"x": a["x"], "attn_w": np.stack(attn_w), "mlp_w": np.stack(mlp_w), "const_w": const_w,
              "w1": a["L0_ffn_w1"], "w2": a["L0_ffn_w2"]}
    nc = bacc.Bacc("TRN2", target_bir_lowering=False, num_devices=1)
    args = [nc.dram_tensor(n, v.shape, mybir.dt.from_np(v.dtype), kind="ExternalInput").ap() for n, v in arrays.items()]
    out = nc.dram_tensor("out", (B, NTOK, D), F32, kind="ExternalOutput").ap()
    build(nc, *args, out)
    r = run_bass_kernel_spmd(nc, [arrays], core_ids=[0])
    return r.results[0]["out"]
```

```python
from contextlib import ExitStack

import numpy as np

import concourse.bass as bass
from concourse import mybir

F32 = mybir.dt.float32
F32R = mybir.dt.float32r
I32 = mybir.dt.int32
U32 = mybir.dt.uint32
ACT = mybir.ActivationFunctionType
ALU = mybir.AluOpType
AX = mybir.AxisListType.X

P = 128
D = 128
B = 64
IMG = 224
PATCH = 16
GRID = IMG // PATCH
NTOK = GRID * GRID + 1
NPAD = NTOK + 1
BOTH = 2 * NPAD
TILES = ((0, P), (P, NTOK - P))
LAYERS = 4
HEADS = 8
NPAIR = HEADS // 2
HD = D // HEADS
STRIP = 2 * HD
HID = 256
HC = HID // P
EXPERTS = 8
FF = 512
FC = FF // P
EPS = 1e-5
SCALE = HD ** -0.5
GROUPS = (0, 1)
SLOTS = (0, 1, 2, 3)
ROUNDS = B // len(SLOTS)
HALF = PATCH // 2
XROWS = 3 * PATCH
XSHIFT = 64
MASKED = -1.0e30
VSTEP = 80

L_WQ = 0
L_WK = L_WQ + D
L_WV = L_WK + D
L_WP = L_WV + D
L_W1 = L_WP + D
L_W2 = L_W1 + HID
L_BV = L_W2 + HC * D
L_BP = L_BV + D
L_B2 = L_BP + D
L_LN1 = L_B2 + D
L_LN2 = L_LN1 + 2
L_BQ = L_LN2 + 2
L_BK = L_BQ + 1
L_B1 = L_BK + 1
L_N = L_B1 + HC
C_CONV = 0
C_FWQ = C_CONV + HALF * D
C_FWQS = C_FWQ + D
C_FWK = C_FWQS + D
C_FWKS = C_FWK + D
C_FWV = C_FWKS + D
C_FWO = C_FWV + D
C_RQ = C_FWO + D
C_RK = C_RQ + D
C_RV = C_RK + D
C_RO = C_RV + D
C_ROUT = C_RO + D
C_NW = C_ROUT + EXPERTS
C_NB = C_NW + D
C_POS = C_NB + D
C_COS = C_POS + NTOK
C_SIN = C_COS + NPAD
C_FW1 = C_SIN + NPAD
C_FW2 = C_FW1 + 1
C_CONVB = C_FW2 + 1
C_CLS = C_CONVB + 1
C_DECAY = C_CLS + 1
C_SCALE = C_DECAY + 1
C_N = C_SCALE + 1

NORMS = 2 * LAYERS + 5
TURNS = 2 * LAYERS + 3
ATTNS = LAYERS + 1
ROPE = LAYERS
N_FINAL, N_RET, N_X, N_RMS1, N_RMS2 = range(2 * LAYERS, NORMS)
T_RET, T_RMS1, T_RMS2 = range(2 * LAYERS, TURNS)

FRONT = ("stat", "norm", "turn", "proj", "split", "stack0", "stack1", "rows0", "rows1", "rows2", "rows3", "rows4",
         "rows5", "rows6", "rows7", "place")
BACK = ("scores0", "scores1", "scores2", "scores3", "sums", "invert", "attend", "normalise", "out", "add", "stat2",
        "norm2", "turn2", "up", "down", "add2")
RETENTION = ("final_stat", "final_norm", "final_scale", "ret_stat", "ret_norm", "ret_turn", "ret_proj", "ret_scores",
             "ret_read", "ret_out")
ROPE_FRONT = ("x_stat", "x_norm", "rms1_stat", "rms1_norm", "rms1_turn", "rope_proj", "rope_turn", "stack0",
              "stack1", "rows0", "rows1", "rows2", "rows3", "rows4", "rows5", "rows6", "rows7", "place")
ROPE_BACK = ("scores0", "scores1", "scores2", "scores3", "sums", "invert", "attend", "normalise", "out", "add",
             "rms2_stat", "rms2_norm", "rms2_turn", "route")
START = "000010101001000100011010010"
LAYER = "1101101101101000011001100101101101111010100110001010000011010010"
REST = ("110110110110100101001101000111011010010100111101110001010010110110110101010101000001000110"
        "11011100101110010100001111010111011")


def group_steps(g):
    names = [(name, 0) for name in ("embed", "embed_turn")]
    for l in range(LAYERS):
        names += [(name, l) for name in FRONT + BACK]
    names += [(name, 0) for name in RETENTION] + [(name, ROPE) for name in ROPE_FRONT + ROPE_BACK]
    return [(name, l, g) for name, l in names]


def make_schedule():
    rest = [group_steps(g) for g in GROUPS]
    out = [rest[int(g)].pop(0) for g in START + (LAYERS - 1) * LAYER + REST]
    assert rest == [[], []]
    return out


SCHEDULE = make_schedule()


def slots_of(group):
    return (2 * group, 2 * group + 1)


def nth(start, n, s):
    return start + (2 * n + s % 2 + 1)


def build(nc, x, tower_w, const_w, sel_w, w1, w2, out):
    with ExitStack() as ctx:
        def sb(name, shape, dt=F32):
            return ctx.enter_context(nc.sbuf_tensor(name, shape, dt))

        def per_slot(name, shape, dt=F32):
            return [sb(f"{name}{s}", shape, dt) for s in SLOTS]

        def sem(name):
            return ctx.enter_context(nc.semaphore(name))

        def per_group(name):
            return [sem(f"{name}_g{g}") for g in GROUPS]

        tw = sb("tw", [P, LAYERS, L_N])
        cw = sb("cw", [P, C_N])
        up_w = sb("up_w", [P, FF])
        down_w = sb("down_w", [P, FC, D])
        ident = sb("ident", [P, P])
        ident_r = sb("ident_r", [P, P], F32R)
        sel = sb("sel", [P, 4, NPAIR, P], F32R)
        sel_row = sb("sel_row", [P, NPAIR, P], F32R)
        causal_r = sb("causal_r", [P, 2, NPAD], F32R)
        den_ones = sb("den_ones", [P, 2, STRIP])
        decay_t = sb("decay_t", [P, 2, NPAD])
        expert_i = sb("expert_i", [P, EXPERTS], I32)
        expert_f = sb("expert_f", [P, EXPERTS])
        mhalf = sb("mhalf", [P, 2])
        eps2 = sb("eps2", [P, 2])
        carrier = sb("carrier", [P, 20])
        lnd = sb("lnd", [P, 6])

        prob = per_slot("prob", [P, 2 * NPAIR * BOTH])
        h = per_slot("h", [P, 2, D])
        hh = per_slot("hh", [P, 2, D])
        yn = per_slot("yn", [P, 2, D])
        yT = per_slot("yT", [P, NPAD])
        oT = per_slot("oT", [P, NTOK])
        work = per_slot("work", [P, 2, BOTH])
        qk_hi = per_slot("qk_hi", [P, 2, NPAD], F32R)
        qk_lo = per_slot("qk_lo", [P, 2, NPAD], F32R)
        k_st = per_slot("k_st", [P, NPAIR, NPAD], F32R)
        q_mask = per_slot("q_mask", [P, NPAIR, 2, NPAD], F32R)
        vpad = per_slot("vpad", [P, 2, NPAIR, VSTEP])
        neg_max = per_slot("neg_max", [P, 12 + P], F32R)
        maxT = per_slot("maxT", [P, BOTH], F32R)
        stats = per_slot("stats", [P, 2, 6])
        mv = per_slot("mv", [P, 2, 2])
        ve = per_slot("ve", [P, 2])
        rstd = per_slot("rstd", [P, 2])
        logit = per_slot("logit", [P, 2, EXPERTS])
        top = per_slot("top", [P, 2, EXPERTS])
        topi = per_slot("topi", [P, 2, EXPERTS], U32)
        topf = per_slot("topf", [P, 2, 2])
        gap = per_slot("gap", [P, 2])
        second = per_slot("second", [P, 2])
        den = per_slot("den", [P, 2])
        gate = per_slot("gate", [P, 2, 2])
        gates = per_slot("gates", [P, 2, EXPERTS])
        gates2 = per_slot("gates2", [P, 2, EXPERTS])

        def img(s):
            return prob[s][:, 0:GRID * IMG].rearrange("p (g w) -> p g w", w=IMG)

        def prob_of(s, t):
            n = NPAIR * BOTH
            return prob[s][:, t * n:(t + 1) * n].rearrange("p (u b) -> p u b", b=BOTH)

        psum = ctx.enter_context(nc.psum_tensor("psum", [P, 8, 512], F32))

        def bank(s, j):
            return psum[:, 2 * s + j, :]

        def pair_in(s, j):
            return bank(s, j)[:, 0:BOTH]

        const_loaded = sem("const_loaded")
        up_loaded = sem("up_loaded")
        down_loaded = sem("down_loaded")
        img_loaded = per_group("img_loaded")
        h_free = per_group("h_free")
        pool_set = sem("pool_set")
        dve_set = sem("dve_set")
        act_set = sem("act_set")
        patches = per_group("patches")
        embedded = per_group("embedded")
        embedded_tok = per_group("embedded_tok")
        h_start = per_group("h_start")
        stats_ready = per_group("stats_ready")
        mean_ready = per_group("mean_ready")
        moments = per_group("moments")
        eps_added = per_group("eps_added")
        rstd_ready = per_group("rstd_ready")
        normed = per_group("normed")
        turned = per_group("turned")
        yT_ready = per_group("yT_ready")
        scaled_tok = per_group("scaled_tok")
        qk_ready = per_group("qk_ready")
        v_ready = per_group("v_ready")
        hi_ready = per_group("hi_ready")
        lo_ready = per_group("lo_ready")
        v_padded = per_group("v_padded")
        stacked = per_group("stacked")
        q_masked = per_group("q_masked")
        k_stacked = per_group("k_stacked")
        rows_ready = per_group("rows_ready")
        max_ready = per_group("max_ready")
        max_placed = per_group("max_placed")
        maxT_ready = per_group("maxT_ready")
        scores_ready = per_group("scores_ready")
        prob_ready = per_group("prob_ready")
        causal_done = per_group("causal_done")
        summed = per_group("summed")
        attended = per_group("attended")
        den_ready = per_group("den_ready")
        oT_ready = per_group("oT_ready")
        proj_ready = per_group("proj_ready")
        bias_added = per_group("bias_added")
        attn_added = per_group("attn_added")
        up_ready = per_group("up_ready")
        gelu_ready = per_group("gelu_ready")
        down_ready = per_group("down_ready")
        mlp_bias = per_group("mlp_bias")
        mlp_added = per_group("mlp_added")
        ret_qkv = per_group("ret_qkv")
        ret_qk = per_group("ret_qk")
        ret_v = per_group("ret_v")
        ret_scored = per_group("ret_scored")
        ret_weighted = per_group("ret_weighted")
        ret_sum = per_group("ret_sum")
        ret_turned = per_group("ret_turned")
        ret_ready = per_group("ret_ready")
        ret_added = per_group("ret_added")
        cos_done = per_group("cos_done")
        rotated = per_group("rotated")
        logits_ready = per_group("logits_ready")
        routing = per_group("routing")
        gap_ready = per_group("gap_ready")
        second_ready = per_group("second_ready")
        sum_ready = per_group("sum_ready")
        ex_up = per_group("ex_up")
        ex_gelu = per_group("ex_gelu")
        ex_down = per_group("ex_down")
        ex_added = per_group("ex_added")

        block = ctx.enter_context(nc.Block())

        @block.sync
        def _(sp):
            def load_images(rnd, g):
                for s in slots_of(g):
                    for c in range(3):
                        src = x[bass.ds(rnd * len(SLOTS) + s, 1), c, :, :].rearrange(
                            "o (g py) w -> py (o g) w", py=PATCH)
                        lo, hi = c * PATCH, (c + 1) * PATCH
                        sp.dma_start(img(s)[lo:hi, :, :], src).then_inc(img_loaded[g], 16)
                        sp.dma_start(img(s)[XSHIFT + lo:XSHIFT + hi, :, 0:IMG - HALF],
                                     src[:, :, HALF:IMG]).then_inc(img_loaded[g], 16)

            def load_up(e):
                sp.dma_start(up_w[:, :], w1[bass.ds(e, 1), :, :].rearrange("o d f -> d (o f)")).then_inc(up_loaded, 16)

            def load_down(e):
                sp.dma_start(down_w[:, :, :], w2[bass.ds(e, 1), :, :].rearrange(
                    "o (c p) d -> p (o c) d", p=P)).then_inc(down_loaded, 16)

            sp.dma_start(prob[3][:, 0:4 * NPAIR * P], sel_w[:, :]).then_inc(const_loaded, 16)
            sp.dma_start(cw[:, :], const_w[:, :]).then_inc(const_loaded, 16)
            sp.dma_start(tw[:, :, :], tower_w[:, :, :]).then_inc(const_loaded, 16)
            sp.wait_ge(pool_set, 1)
            load_images(0, 0)
            load_up(0)
            load_down(0)
            sp.wait_ge(dve_set, 1)
            load_images(0, 1)
            with sp.Fori(0, ROUNDS) as i:
                coming = sp.snap((i + 1) % ROUNDS)
                for g in GROUPS:
                    sp.wait_ge(attended[g], i * (2 * ATTNS) + 2 * ATTNS)
                    load_images(coming, g)
                with sp.Fori(0, EXPERTS) as e:
                    done = sp.snap((i * EXPERTS + e) * 2 + 2)
                    following = sp.snap((e + 1) % EXPERTS)
                    for g in GROUPS:
                        sp.wait_ge(ex_up[g], done)
                    load_up(following)
                    for g in GROUPS:
                        sp.wait_ge(ex_down[g], done)
                    load_down(following)
                for g in GROUPS:
                    sp.wait_ge(ex_added[g], (i + 1) * (2 * (EXPERTS + 1)))
                    for s in slots_of(g):
                        for t, (t0, m) in enumerate(TILES):
                            sp.dma_start(out[bass.ds(i * len(SLOTS) + s, 1), t0:t0 + m, :].rearrange(
                                "o t d -> t (o d)"), h[s][0:m, t, :]).then_inc(h_free[g], 16)
            for g in GROUPS:
                sp.wait_ge(h_free[g], 64 * (ROUNDS + 1))
                sp.wait_ge(img_loaded[g], 192 * (ROUNDS + 1))
            sp.wait_ge(up_loaded, 16 * (ROUNDS * EXPERTS + 1))
            sp.wait_ge(down_loaded, 16 * (ROUNDS * EXPERTS + 1))

        @block.tensor
        def _(pe):
            mm = nc.tensor.matmul
            pe.wait_ge(const_loaded, 48)
            pe.wait_ge(pool_set, 2)
            pe.wait_ge(dve_set, 1)
            with pe.Fori(0, ROUNDS) as i:
                once = pe.snap(i * 2)
                norms = pe.snap(i * (2 * NORMS))
                turns = pe.snap(i * (2 * TURNS))
                attns = pe.snap(i * (2 * ATTNS))
                halves = pe.snap(i * (2 * ATTNS * 2))
                eighths = pe.snap(i * (2 * ATTNS * 8))
                layers = pe.snap(i * (2 * LAYERS))

                def to_tokens(s, j, lhsT, w):
                    for t, (t0, m) in enumerate(TILES):
                        last = mm(bank(s, j)[0:m, t * D:(t + 1) * D], lhsT[:, t0:t0 + m], w, start=True, stop=True)
                    return last

                def weights(l, first):
                    return tw[:, l, first:first + D]

                def embed(l, g):
                    pe.wait_ge(h_free[g], i * 64 + 64)
                    pe.wait_ge(img_loaded[g], i * 192 + 192)
                    for s in slots_of(g):
                        for px in range(HALF):
                            last = mm(bank(s, 0)[:, 0:NTOK - 1], cw[:, C_CONV + px * D:C_CONV + (px + 1) * D],
                                      img(s)[:, :, px:IMG:PATCH], start=(px == 0), stop=(px == HALF - 1))
                        last.then_inc(patches[g], 1)

                def embed_turn(l, g):
                    for s in slots_of(g):
                        pe.wait_ge(embedded[g], nth(once, 0, s))
                        for t, (t0, m) in enumerate(TILES):
                            last = nc.tensor.transpose(bank(s, 1)[0:m, t * D:(t + 1) * D], oT[s][:, t0:t0 + m],
                                                       ident[:, :])
                        last.then_inc(embedded_tok[g], 1)

                def turn(g, n):
                    for s in slots_of(g):
                        pe.wait_ge(normed[g], nth(norms, n, s))
                        for t, (t0, m) in enumerate(TILES):
                            last = nc.tensor.transpose(bank(s, 1)[:, t0:t0 + m], yn[s][0:m, t, :], ident[0:m, 0:m])
                        last.then_inc(turned[g], 1)

                def proj(l, g):
                    for s in slots_of(g):
                        pe.wait_ge(yT_ready[g], nth(turns, 2 * l, s))
                        mm(bank(s, 0)[:, 0:NPAD], weights(l, L_WQ), yT[s][:, :], start=True, stop=True)
                        mm(bank(s, 0)[:, NPAD:BOTH], weights(l, L_WK), yT[s][:, :], start=True,
                           stop=True).then_inc(qk_ready[g], 1)
                        to_tokens(s, 1, yT[s], weights(l, L_WV)).then_inc(v_ready[g], 1)

                def stack(l, g, half):
                    for s in slots_of(g):
                        if half == 0:
                            pe.wait_ge(lo_ready[g], nth(attns, l, s))
                        for j in range(2):
                            if half == 0 and j == 1:
                                pe.wait_ge(v_padded[g], nth(attns, l, s))
                            if half == 1:
                                read = (q_masked, k_stacked)[j]
                                pe.wait_ge(read[g], nth(halves, 2 * l, s))
                            for c in range(2):
                                dst = bank(s, j)[:, c * NPAD:(c + 1) * NPAD]
                                mm(dst, sel[:, 2 * j, 2 * half + c, :], qk_hi[s][:, j, :], start=True, stop=False)
                                last = mm(dst, sel[:, 2 * j + 1, 2 * half + c, :], qk_lo[s][:, j, :], start=False,
                                          stop=True)
                        last.then_inc(stacked[g], 1)

                def rows(l, g, n):
                    t, u = divmod(n, NPAIR)
                    t0, m = TILES[t]
                    for s in slots_of(g):
                        if n == 0:
                            pe.wait_ge(q_masked[g], nth(halves, 2 * l + 1, s))
                            pe.wait_ge(k_stacked[g], nth(halves, 2 * l + 1, s))
                        if n >= 2:
                            pe.wait_ge(max_ready[g], nth(eighths, 8 * l + n - 2, s))
                        for par in range(2):
                            dst = bank(s, u % 2)[0:m, par * NPAD:(par + 1) * NPAD]
                            if l == ROPE:
                                mm(dst, ident_r[:, 0:m], causal_r[:, t, :], start=True, stop=False)
                            last = mm(dst, q_mask[s][:, u, par, t0:t0 + m], k_st[s][:, u, :],
                                      start=(l != ROPE), stop=True)
                        last.then_inc(rows_ready[g], 1)

                def place(l, g):
                    for s in slots_of(g):
                        pe.wait_ge(max_ready[g], nth(eighths, 8 * l + 7, s))
                        for par in range(2):
                            for t, (t0, m) in enumerate(TILES):
                                c = 4 * (2 * t + par)
                                n = m + m % 2
                                last = mm(bank(s, 0)[:, par * NPAD + t0:par * NPAD + t0 + n],
                                          neg_max[s][0:m, c:c + P], ident_r[0:m, 0:n], start=True, stop=True)
                        last.then_inc(max_placed[g], 1)

                def scores(l, g, k):
                    for n in (2 * k, 2 * k + 1):
                        t, u = divmod(n, NPAIR)
                        t0, m = TILES[t]
                        for s in slots_of(g):
                            if n < 2:
                                pe.wait_ge(maxT_ready[g], nth(attns, l, s))
                            else:
                                pe.wait_ge(prob_ready[g], nth(eighths, 8 * l + n - 2, s))
                            dst = pair_in(s, u % 2)[0:m, :]
                            mm(dst, k_st[s][:, u, t0:t0 + m], q_mask[s][:, u, :, :].rearrange("p a n -> p (a n)"),
                               start=True, stop=False)
                            mm(dst, sel_row[:, u, 0:m], maxT[s][:, :], start=False,
                               stop=True).then_inc(scores_ready[g], 1)

                def weighted(s, j, values):
                    for t, (t0, m) in enumerate(TILES):
                        for par in range(2):
                            for u in range(NPAIR):
                                last = mm(bank(s, j)[STRIP * u:STRIP * (u + 1), 0:NTOK], values(t, m, par, u),
                                          prob_of(s, t)[0:m, u, par * NPAD:par * NPAD + NTOK],
                                          start=(t == par == 0), stop=(t == par == 1))
                    return last

                def sums(l, g):
                    for s in slots_of(g):
                        pe.wait_ge(prob_ready[g], nth(eighths, 8 * l + 7, s))
                        if l == ROPE:
                            pe.wait_ge(causal_done[g], nth(once * 2, 1, s))
                        weighted(s, 1, lambda t, m, par, u: den_ones[0:m, par, :]).then_inc(summed[g], 1)

                def attend(l, g):
                    for s in slots_of(g):
                        weighted(s, 0, lambda t, m, par, u: vpad[s][0:m, t, u, 48 * par:48 * par + STRIP]
                                 ).then_inc(attended[g], 1)

                def out_proj(l, g):
                    w = weights(l, L_WP) if l < LAYERS else cw[:, C_FWO:C_FWO + D]
                    for s in slots_of(g):
                        pe.wait_ge(oT_ready[g], nth(attns, l, s))
                        to_tokens(s, 0, oT[s], w).then_inc(proj_ready[g], 1)

                def up(l, g):
                    for s in slots_of(g):
                        pe.wait_ge(yT_ready[g], nth(turns, 2 * l + 1, s))
                        for c in range(HC):
                            last = mm(bank(s, 0)[:, c * NPAD:c * NPAD + NTOK], weights(l, L_W1 + c * P),
                                      yT[s][:, 0:NTOK], start=True, stop=True)
                        last.then_inc(up_ready[g], 1)

                def down(l, g):
                    for s in slots_of(g):
                        pe.wait_ge(gelu_ready[g], nth(layers, l, s))
                        for t, (t0, m) in enumerate(TILES):
                            for c in range(HC):
                                last = mm(bank(s, 1)[0:m, t * D:(t + 1) * D],
                                          work[s][:, 0, c * NPAD + t0:c * NPAD + t0 + m], weights(l, L_W2 + c * D),
                                          start=(c == 0), stop=(c == HC - 1))
                        last.then_inc(down_ready[g], 1)

                def ret_proj(l, g):
                    for s in slots_of(g):
                        pe.wait_ge(yT_ready[g], nth(turns, T_RET, s))
                        mm(bank(s, 0)[:, 0:NTOK], cw[:, C_RQ:C_RQ + D], yT[s][:, 0:NTOK], start=True, stop=True)
                        mm(bank(s, 0)[:, NPAD:NPAD + NTOK], cw[:, C_RK:C_RK + D], yT[s][:, 0:NTOK], start=True,
                           stop=True)
                        to_tokens(s, 1, yT[s], cw[:, C_RV:C_RV + D]).then_inc(ret_qkv[g], 1)

                def ret_scores(l, g):
                    for s in slots_of(g):
                        pe.wait_ge(ret_qk[g], nth(once, 0, s))
                        pe.wait_ge(ret_v[g], nth(once, 0, s))
                        for t, (t0, m) in enumerate(TILES):
                            last = mm(bank(s, 0)[0:m, t * NPAD:t * NPAD + NTOK], work[s][:, 0, NPAD + t0:NPAD + t0 + m],
                                      work[s][:, 0, 0:NTOK], start=True, stop=True)
                        last.then_inc(ret_scored[g], 1)

                def ret_read(l, g):
                    for s in slots_of(g):
                        pe.wait_ge(ret_weighted[g], nth(once, 0, s))
                        for t, (t0, m) in enumerate(TILES):
                            last = mm(bank(s, 1)[:, 0:NTOK], yn[s][0:m, t, :],
                                      work[s][0:m, 1, t * NPAD:t * NPAD + NTOK], start=(t == 0), stop=(t == 1))
                        last.then_inc(ret_sum[g], 1)

                def ret_out(l, g):
                    for s in slots_of(g):
                        pe.wait_ge(ret_turned[g], nth(once, 0, s))
                        to_tokens(s, 0, oT[s], cw[:, C_RO:C_RO + D]).then_inc(ret_ready[g], 1)

                def rope_proj(l, g):
                    for s in slots_of(g):
                        pe.wait_ge(yT_ready[g], nth(turns, T_RMS1, s))
                        for j, cols in enumerate(((C_FWQ, C_FWQS), (C_FWK, C_FWKS))):
                            for k, col in enumerate(cols):
                                last = mm(bank(s, j)[:, k * NPAD:(k + 1) * NPAD], cw[:, col:col + D], yT[s][:, :],
                                          start=True, stop=True)
                        last.then_inc(qk_ready[g], 1)

                def rope_v(l, g):
                    for s in slots_of(g):
                        pe.wait_ge(cos_done[g], nth(once, 0, s))
                        to_tokens(s, 1, yT[s], cw[:, C_FWV:C_FWV + D]).then_inc(v_ready[g], 1)

                def logits(l, g):
                    for s in slots_of(g):
                        pe.wait_ge(yT_ready[g], nth(turns, T_RMS2, s))
                        for t, (t0, m) in enumerate(TILES):
                            last = mm(bank(s, 1)[0:m, t * EXPERTS:(t + 1) * EXPERTS], yT[s][:, t0:t0 + m],
                                      cw[:, C_ROUT:C_ROUT + EXPERTS], start=True, stop=True)
                        last.then_inc(logits_ready[g], 1)

                part = {
                    "embed": embed, "embed_turn": embed_turn, "turn": lambda l, g: turn(g, 2 * l), "proj": proj,
                    "stack0": lambda l, g: stack(l, g, 0), "stack1": lambda l, g: stack(l, g, 1),
                    **{f"rows{n}": lambda l, g, n=n: rows(l, g, n) for n in range(8)}, "place": place,
                    "scores0": lambda l, g: scores(l, g, 0), "scores1": lambda l, g: scores(l, g, 1),
                    "scores2": lambda l, g: scores(l, g, 2), "scores3": lambda l, g: scores(l, g, 3),
                    "sums": sums, "attend": attend, "out": out_proj, "turn2": lambda l, g: turn(g, 2 * l + 1), "up": up,
                    "down": down, "ret_turn": lambda l, g: turn(g, N_RET), "ret_proj": ret_proj,
                    "ret_scores": ret_scores, "ret_read": ret_read, "ret_out": ret_out,
                    "rms1_turn": lambda l, g: turn(g, N_RMS1), "rope_proj": rope_proj, "rope_turn": rope_v,
                    "rms2_turn": lambda l, g: turn(g, N_RMS2), "route": logits,
                }
                for name, l, g in SCHEDULE:
                    if name in part:
                        part[name](l, g)

                with pe.Fori(0, EXPERTS) as e:
                    expert = pe.snap((i * EXPERTS + e) * 2)
                    added = pe.snap((i * (EXPERTS + 1) + e) * 2)
                    load_n = pe.snap((i * EXPERTS + e) * 16 + 16)
                    pe.wait_ge(up_loaded, load_n)
                    for s in SLOTS:
                        pe.wait_ge(ex_added[s // 2], nth(added, 0, s))
                        for c in range(FC):
                            last = mm(bank(s, c // 2)[:, c % 2 * NPAD:c % 2 * NPAD + NTOK],
                                      up_w[:, c * P:(c + 1) * P], yT[s][:, 0:NTOK], start=True, stop=True)
                        last.then_inc(ex_up[s // 2], 1)
                    pe.wait_ge(down_loaded, load_n)
                    for s in SLOTS:
                        pe.wait_ge(ex_gelu[s // 2], nth(expert, 0, s))
                        for t, (t0, m) in enumerate(TILES):
                            for c in range(FC):
                                last = mm(bank(s, 0)[0:m, t * D:(t + 1) * D],
                                          work[s][:, c // 2, c % 2 * NPAD + t0:c % 2 * NPAD + t0 + m],
                                          down_w[:, c, :], start=(c == 0), stop=(c == FC - 1))
                        last.then_inc(ex_down[s // 2], 1)

        @block.scalar
        def _(act):
            run = nc.scalar.activation
            act.wait_ge(dve_set, 3)
            run(lnd[:, 2:3], lnd[:, 1:2], ACT.Exp).then_inc(act_set, 1)
            act.wait_ge(act_set, 1)
            run(lnd[:, 3:4], lnd[:, 2:3], ACT.Ln, bias=1.0).then_inc(act_set, 1)
            act.wait_ge(dve_set, 5)
            run(decay_t[:, :, :], decay_t[:, :, :], ACT.Exp, scale=lnd[:, 5:6]).then_inc(act_set, 1)
            with act.Fori(0, ROUNDS) as i:
                once = act.snap(i * 2)
                turns = act.snap(i * (2 * TURNS))
                attns = act.snap(i * (2 * ATTNS))
                halves = act.snap(i * (2 * ATTNS * 2))
                eighths = act.snap(i * (2 * ATTNS * 8))
                layers = act.snap(i * (2 * LAYERS))

                def to_yT(g, n, scale=None, bias=None):
                    kw = {k: v for k, v in (("scale", scale), ("bias", bias)) if v is not None}
                    for s in slots_of(g):
                        act.wait_ge(turned[g], nth(turns, n, s))
                        run(yT[s][:, 0:NTOK], bank(s, 1)[:, 0:NTOK], ACT.Identity if kw else ACT.Copy,
                            **kw).then_inc(yT_ready[g], 1)

                def column(l, c):
                    return tw[:, l, c:c + 1]

                def hi(l, g):
                    for s in slots_of(g):
                        act.wait_ge(qk_ready[g], nth(attns, l, s))
                        for j, c in enumerate((L_BQ, L_BK)):
                            last = run(qk_hi[s][:, j, :], bank(s, 0)[:, j * NPAD:(j + 1) * NPAD], ACT.Identity,
                                       bias=column(l, c))
                        last.then_inc(hi_ready[g], 1)

                def rope_hi(l, g):
                    for s in slots_of(g):
                        act.wait_ge(rotated[g], nth(once, 0, s))
                        run(qk_hi[s][:, :, :], work[s][:, 0, :].rearrange("p (j n) -> p j n", j=2),
                            ACT.Copy).then_inc(hi_ready[g], 1)

                def mask_q(l, g, half):
                    for s in slots_of(g):
                        act.wait_ge(stacked[g], nth(halves, 2 * l + half, s))
                        for par in range(2):
                            rows = slice(64 * par, 64 * par + 64)
                            last = run(q_mask[s][rows, 2 * half:2 * half + 2, par, :],
                                       pair_in(s, 0)[rows, :].rearrange("p (c n) -> p c n", c=2), ACT.Copy)
                        last.then_inc(q_masked[g], 1)

                def exps(l, g, k):
                    for n in (2 * k, 2 * k + 1):
                        t, u = divmod(n, NPAIR)
                        m = TILES[t][1]
                        for s in slots_of(g):
                            act.wait_ge(scores_ready[g], nth(eighths, 8 * l + n, s))
                            run(prob_of(s, t)[0:m, u, :], pair_in(s, u % 2)[0:m, :], ACT.Exp,
                                scale=SCALE).then_inc(prob_ready[g], 1)

                def gelu(l, g):
                    for s in slots_of(g):
                        act.wait_ge(up_ready[g], nth(layers, l, s))
                        for c in range(HC):
                            cols = slice(c * NPAD, c * NPAD + NTOK)
                            last = run(work[s][:, 0, cols], bank(s, 0)[:, cols], ACT.Gelu, bias=column(l, L_B1 + c))
                        last.then_inc(gelu_ready[g], 1)

                def ret_keep_qk(l, g):
                    for s in slots_of(g):
                        act.wait_ge(ret_qkv[g], nth(once, 0, s))
                        run(work[s][:, 0, :].rearrange("p (j n) -> p j n", j=2)[:, :, 0:NTOK],
                            pair_in(s, 0).rearrange("p (j n) -> p j n", j=2)[:, :, 0:NTOK],
                            ACT.Copy).then_inc(ret_qk[g], 1)

                def ret_turn(l, g):
                    for s in slots_of(g):
                        act.wait_ge(ret_sum[g], nth(once, 0, s))
                        run(oT[s][:, :], bank(s, 1)[:, 0:NTOK], ACT.Copy).then_inc(ret_turned[g], 1)

                def second_gate(l, g):
                    for s in slots_of(g):
                        act.wait_ge(gap_ready[g], nth(once, 0, s))
                        run(second[s][:, :], gap[s][:, :], ACT.Exp).then_inc(second_ready[g], 1)

                part = {
                    "turn": lambda l, g: to_yT(g, 2 * l, column(l, L_LN1), column(l, L_LN1 + 1)), "proj": hi,
                    "stack0": lambda l, g: mask_q(l, g, 0), "stack1": lambda l, g: mask_q(l, g, 1),
                    "scores0": lambda l, g: exps(l, g, 0), "scores1": lambda l, g: exps(l, g, 1),
                    "scores2": lambda l, g: exps(l, g, 2), "scores3": lambda l, g: exps(l, g, 3),
                    "turn2": lambda l, g: to_yT(g, 2 * l + 1, column(l, L_LN2), column(l, L_LN2 + 1)), "up": gelu,
                    "ret_turn": lambda l, g: to_yT(g, T_RET), "ret_proj": ret_keep_qk, "ret_read": ret_turn,
                    "rms1_turn": lambda l, g: to_yT(g, T_RMS1, cw[:, C_FW1:C_FW1 + 1]), "rope_turn": rope_hi,
                    "rms2_turn": lambda l, g: to_yT(g, T_RMS2, cw[:, C_FW2:C_FW2 + 1]), "route": second_gate,
                }
                for name, l, g in SCHEDULE:
                    if name in part:
                        part[name](l, g)

                with act.Fori(0, EXPERTS) as e:
                    expert = act.snap((i * EXPERTS + e) * 2)
                    for s in SLOTS:
                        act.wait_ge(ex_up[s // 2], nth(expert, 0, s))
                        run(work[s][:, :, :].rearrange("p a (c n) -> p a c n", c=2)[:, :, :, 0:NTOK],
                            psum[:, 2 * s:2 * s + 2, 0:BOTH].rearrange("p a (c n) -> p a c n", c=2)[:, :, :, 0:NTOK],
                            ACT.Gelu).then_inc(ex_gelu[s // 2], 1)

        @block.gpsimd
        def _(pool):
            for s in SLOTS:
                first = 4 * NPAIR * P if s == SLOTS[-1] else 0
                last = nc.gpsimd.memset(prob[s][:, first:], 0.0)
            last.then_inc(pool_set, 1)
            for s in SLOTS:
                for a in (hh, yn, yT, stats, mv, ve, gap, gates, gates2, logit, den, second, vpad, topf, gate, top,
                          rstd, work):
                    nc.gpsimd.memset(a[s][:], 0.0)
                nc.gpsimd.memset(h[s][:, :, :], 0.0).then_inc(h_free[s // 2], 32)
            nc.gpsimd.memset(mhalf[:, :], -0.5)
            nc.gpsimd.memset(eps2[:, :], EPS)
            nc.gpsimd.memset(den_ones[:, :, :], 0.0)
            nc.gpsimd.iota(expert_i[:, :], pattern=[[1, EXPERTS]], base=0, channel_multiplier=0)
            nc.gpsimd.memset(ident[:, :], 0.0).then_inc(pool_set, 1)
            pool.wait_ge(pool_set, 2)
            for par in range(2):
                nc.gpsimd.memset(den_ones[:, par, par * HD:(par + 1) * HD], 1.0)
            for t, (t0, _) in enumerate(TILES):
                nc.gpsimd.iota(work[1][:, 0, t * NPAD:(t + 1) * NPAD].bitcast(I32), pattern=[[-1, NPAD]], base=t0 - 1,
                               channel_multiplier=1)
                m = work[0][:, 0, t * NPAD:(t + 1) * NPAD]
                nc.gpsimd.affine_select(out=m, in_=m, pattern=[[-1, NPAD]], compare_op=ALU.is_ge, fill=MASKED,
                                        base=t0, channel_multiplier=1)
            for u in range(NPAIR):
                m = work[2][:, 0, 0:P] if u == 0 else yn[u][:, 0, :]
                nc.gpsimd.affine_select(out=m, in_=m, pattern=[[0, P]], compare_op=ALU.not_equal, fill=1.0,
                                        base=-u, channel_multiplier=1)
            nc.gpsimd.affine_select(out=ident[:, :], in_=ident[:, :], pattern=[[-1, P]],
                                    compare_op=ALU.not_equal, fill=1.0, base=0,
                                    channel_multiplier=1).then_inc(pool_set, 1)
            pool.wait_ge(act_set, 3)
            for t, (t0, _) in enumerate(TILES):
                last = nc.gpsimd.affine_select(out=decay_t[:, t, :], in_=decay_t[:, t, :], pattern=[[-1, NPAD]],
                                               compare_op=ALU.is_gt, fill=0.0, base=t0, channel_multiplier=1)
            last.then_inc(pool_set, 1)

            with pool.Fori(0, ROUNDS) as i:
                once = pool.snap(i * 2)
                norms = pool.snap(i * (2 * NORMS))
                eighths = pool.snap(i * (2 * ATTNS * 8))

                def invert(g, n, rms=False):
                    for s in slots_of(g):
                        pool.wait_ge(moments[g], nth(norms, n, s))
                        nc.gpsimd.tensor_tensor(ve[s][:, :], ve[s][:, :] if rms else mv[s][:, :, 1], eps2[:, :],
                                                ALU.add).then_inc(eps_added[g], 1)
                    for s in slots_of(g):
                        pool.wait_ge(eps_added[g], nth(norms, n, s))
                        nc.gpsimd.tensor_tensor(rstd[s][:, :], ve[s][:, :], mhalf[:, :],
                                                ALU.pow).then_inc(rstd_ready[g], 1)

                def add_row(l, g, n, col, added):
                    for s in slots_of(g):
                        pool.wait_ge(normed[g], nth(norms, n, s))
                        for t, (_, m) in enumerate(TILES):
                            last = nc.gpsimd.tensor_tensor(h[s][0:m, t, :], h[s][0:m, t, :],
                                                           tw[0:m, l, col:col + D], ALU.add)
                        last.then_inc(added[g], 1)

                def cut(l, g, t):
                    if l != ROPE:
                        return
                    t0, m = TILES[t]
                    for s in slots_of(g):
                        pool.wait_ge(prob_ready[g], nth(eighths, 8 * l + 4 * t + NPAIR - 1, s))
                        c = 2 * s + t
                        nc.gpsimd.tensor_tensor(carrier[:, c:c + 1], mhalf[:, 0:1], mhalf[:, 0:1], ALU.mult)
                        p = prob_of(s, t)[0:m, :, :].rearrange("p u (a n) -> p (u a) n", n=NPAD)
                        nc.gpsimd.affine_select(out=p, in_=p, pattern=[[0, HEADS], [1, NPAD]],
                                                compare_op=ALU.is_ge, fill=0.0, base=-t0,
                                                channel_multiplier=-1).then_inc(causal_done[g], 1)

                def sum_up(l, g):
                    for s in slots_of(g):
                        pool.wait_ge(normed[g], nth(norms, N_RMS2, s))
                        for t, (_, m) in enumerate(TILES):
                            last = nc.gpsimd.tensor_tensor(h[s][0:m, t, :], h[s][0:m, t, :], hh[s][0:m, t, :],
                                                           ALU.add)
                        last.then_inc(sum_ready[g], 1)

                part = {
                    "stat": lambda l, g: invert(g, 2 * l), "stat2": lambda l, g: invert(g, 2 * l + 1),
                    "norm": lambda l, g: add_row(l, g, 2 * l, L_BP, bias_added),
                    "norm2": lambda l, g: add_row(l, g, 2 * l + 1, L_B2, mlp_bias),
                    "final_stat": lambda l, g: invert(g, N_FINAL), "ret_stat": lambda l, g: invert(g, N_RET),
                    "x_stat": lambda l, g: invert(g, N_X), "rms1_stat": lambda l, g: invert(g, N_RMS1, True),
                    "rms2_stat": lambda l, g: invert(g, N_RMS2, True),
                    "scores1": lambda l, g: cut(l, g, 0), "scores3": lambda l, g: cut(l, g, 1),
                    "rms2_norm": sum_up,
                }
                for name, l, g in SCHEDULE:
                    if name in part:
                        part[name](l, g)

        @block.vector
        def _(dve):
            v = nc.vector
            cleared = (neg_max, q_mask)
            dve.wait_ge(pool_set, 3)
            v.tensor_copy(ident_r[:, :], ident[:, :])
            v.tensor_copy(causal_r[:, :, :], work[0][:, 0, :].rearrange("p (t n) -> p t n", t=2))
            for u in range(NPAIR):
                v.tensor_copy(sel_row[:, u, :], work[2][:, 0, 0:P] if u == 0 else yn[u][:, 0, :])
            v.tensor_copy(expert_f[:, :], expert_i[:, :])
            for s in SLOTS:
                for a in cleared:
                    v.memset(a[s][:].bitcast(U32), 0)
            dve.wait_ge(const_loaded, 48)
            v.tensor_copy(sel[:, :, :, :].rearrange("p a u n -> p (a u n)"),
                          prob[3][:, 0:4 * NPAIR * P]).then_inc(dve_set, 1)
            v.tensor_scalar(cw[:, C_POS + 1:C_POS + NTOK], cw[:, C_POS + 1:C_POS + NTOK], cw[:, C_CONVB:C_CONVB + 1],
                            None, ALU.add)
            v.tensor_scalar(cw[:, C_POS:C_POS + 1], cw[:, C_POS:C_POS + 1], cw[:, C_CLS:C_CLS + 1], None, ALU.add)
            v.tensor_scalar(lnd[:, 0:1], cw[:, C_DECAY:C_DECAY + 1], -1.0, None, ALU.mult).then_inc(dve_set, 1)
            dve.wait_ge(dve_set, 2)
            v.tensor_scalar(lnd[:, 4:5], lnd[:, 0:1], 0.0, None, ALU.max)
            v.tensor_tensor(lnd[:, 1:2], lnd[:, 0:1], cw[:, C_DECAY:C_DECAY + 1], ALU.min).then_inc(dve_set, 1)
            dve.wait_ge(act_set, 2)
            v.scalar_tensor_tensor(lnd[:, 5:6], lnd[:, 3:4], -1.0, lnd[:, 4:5], ALU.mult,
                                   ALU.subtract).then_inc(dve_set, 1)
            v.tensor_scalar(decay_t[:, :, :].rearrange("p t n -> p (t n)"), work[1][:, 0, :].bitcast(I32), 0.0, None,
                            ALU.max).then_inc(dve_set, 1)
            dve.wait_ge(pool_set, 4)
            with dve.Fori(0, ROUNDS) as i:
                once = dve.snap(i * 2)
                twice = dve.snap(i * 4)
                norms = dve.snap(i * (2 * NORMS))
                attns = dve.snap(i * (2 * ATTNS))
                halves = dve.snap(i * (2 * ATTNS * 2))
                eighths = dve.snap(i * (2 * ATTNS * 8))
                layers = dve.snap(i * (2 * LAYERS))
                routes = dve.snap(i * (2 * 9))
                stored = dve.snap(i * 64 + 64)

                def embed(l, g):
                    for s in slots_of(g):
                        dve.wait_ge(patches[g], nth(once, 0, s))
                        v.tensor_copy(oT[s][:, 0:1], cw[:, C_POS:C_POS + 1])
                        v.tensor_tensor(oT[s][:, 1:NTOK], bank(s, 0)[:, 0:NTOK - 1], cw[:, C_POS + 1:C_POS + NTOK],
                                        ALU.add).then_inc(embedded[g], 1)

                def embed_turn(l, g):
                    for s in slots_of(g):
                        dve.wait_ge(embedded_tok[g], nth(once, 0, s))
                        dve.wait_ge(h_free[g], stored)
                        for t, (_, m) in enumerate(TILES):
                            last = v.tensor_copy(h[s][0:m, t, :], bank(s, 1)[0:m, t * D:(t + 1) * D])
                        last.then_inc(h_start[g], 1)

                def moments_of(g, src, n, ready, nth_ready, rms=False):
                    for s in slots_of(g):
                        dve.wait_ge(ready[g], nth(nth_ready[0], nth_ready[1], s))
                        for t, (_, m) in enumerate(TILES):
                            last = v.bn_stats(stats[s][0:m, t, :], src[s][0:m, t, :])
                        last.then_inc(stats_ready[g], 1)
                    for s in slots_of(g):
                        dve.wait_ge(stats_ready[g], nth(norms, n, s))
                        v.memset(carrier[:, 8 + s:9 + s], 0.0)
                        for t, (_, m) in enumerate(TILES):
                            last = v.bn_aggr(mv[s][0:m, t, :], stats[s][0:m, t, :])
                        last.then_inc(mean_ready[g] if rms else moments[g], 1)
                    if rms:
                        for s in slots_of(g):
                            dve.wait_ge(mean_ready[g], nth(twice, (N_RMS1, N_RMS2).index(n), s))
                            for t, (_, m) in enumerate(TILES):
                                last = v.scalar_tensor_tensor(ve[s][0:m, t:t + 1], mv[s][0:m, t, 0:1],
                                                              mv[s][0:m, t, 0:1], mv[s][0:m, t, 1:2], ALU.mult,
                                                              ALU.add)
                            last.then_inc(moments[g], 1)

                def apply(g, src, dst, n, rms=False):
                    for s in slots_of(g):
                        dve.wait_ge(rstd_ready[g], nth(norms, n, s))
                        for t, (_, m) in enumerate(TILES):
                            if rms:
                                last = v.tensor_scalar(dst[s][0:m, t, :], src[s][0:m, t, :], rstd[s][0:m, t:t + 1],
                                                       None, ALU.mult)
                            else:
                                last = v.tensor_scalar(dst[s][0:m, t, :], src[s][0:m, t, :], mv[s][0:m, t, 0:1],
                                                       rstd[s][0:m, t:t + 1], ALU.subtract, ALU.mult)
                        last.then_inc(normed[g], 1)

                def stat(l, g):
                    if l == 0:
                        moments_of(g, h, 0, h_start, (once, 0))
                    else:
                        moments_of(g, h, 2 * l, mlp_added, (layers, l - 1))

                def heads_apart(s, t, m):
                    return (vpad[s][0:m, t, :, :].rearrange("p u (k d) -> p u k d", d=HD)[:, :, 0::4, :],
                            bank(s, 1)[0:m, t * D:(t + 1) * D].rearrange("p (u a d) -> p u a d", a=2, d=HD))

                def split(l, g):
                    bias = tw[:, l, L_BV:L_BV + D].rearrange("p (u a d) -> p u a d", a=2, d=HD)
                    for s in slots_of(g):
                        dve.wait_ge(hi_ready[g], nth(attns, l, s))
                        for j, c in enumerate((L_BQ, L_BK)):
                            last = v.scalar_tensor_tensor(qk_lo[s][:, j, :], bank(s, 0)[:, j * NPAD:(j + 1) * NPAD],
                                                          tw[:, l, c:c + 1], qk_hi[s][:, j, :].bitcast(F32), ALU.add,
                                                          ALU.subtract)
                        last.then_inc(lo_ready[g], 1)
                        dve.wait_ge(v_ready[g], nth(attns, l, s))
                        for t, (_, m) in enumerate(TILES):
                            dst, src = heads_apart(s, t, m)
                            last = v.tensor_tensor(dst, src, bias[0:m], ALU.add)
                        last.then_inc(v_padded[g], 1)

                def rope_rotate(l, g):
                    for s in slots_of(g):
                        dve.wait_ge(qk_ready[g], nth(attns, ROPE, s))
                        for j in range(2):
                            cols = slice(j * NPAD, (j + 1) * NPAD)
                            v.tensor_tensor(work[s][:, 0, cols], bank(s, j)[:, 0:NPAD], cw[:, C_COS:C_COS + NPAD],
                                            ALU.mult)
                            last = v.tensor_tensor(work[s][:, 1, cols], bank(s, j)[:, NPAD:BOTH],
                                                   cw[:, C_SIN:C_SIN + NPAD], ALU.mult)
                        last.then_inc(cos_done[g], 1)
                    for s in slots_of(g):
                        dve.wait_ge(cos_done[g], nth(once, 0, s))
                        v.tensor_tensor(work[s][:, 0, :], work[s][:, 0, :], work[s][:, 1, :],
                                        ALU.add).then_inc(rotated[g], 1)

                def rope_values(l, g):
                    for s in slots_of(g):
                        dve.wait_ge(hi_ready[g], nth(attns, ROPE, s))
                        v.tensor_tensor(qk_lo[s][:, :, :], work[s][:, 0, :].rearrange("p (j n) -> p j n", j=2),
                                        qk_hi[s][:, :, :].bitcast(F32), ALU.subtract).then_inc(lo_ready[g], 1)
                        dve.wait_ge(v_ready[g], nth(attns, ROPE, s))
                        for t, (_, m) in enumerate(TILES):
                            last = v.tensor_copy(*heads_apart(s, t, m))
                        last.then_inc(v_padded[g], 1)

                def keep_k(l, g, half):
                    for s in slots_of(g):
                        dve.wait_ge(stacked[g], nth(halves, 2 * l + half, s))
                        v.tensor_copy(k_st[s][:, 2 * half:2 * half + 2, :],
                                      pair_in(s, 1).rearrange("p (c n) -> p c n", c=2)).then_inc(k_stacked[g], 1)

                def maxima(l, g, n):
                    t, u = divmod(n, NPAIR)
                    m = TILES[t][1]
                    c = 8 * t + u
                    for s in slots_of(g):
                        dve.wait_ge(rows_ready[g], nth(eighths, 8 * l + n, s))
                        v.tensor_reduce(neg_max[s][0:m, c:c + 5:4],
                                        pair_in(s, u % 2)[0:m, :].rearrange("p (a n) -> p a n", a=2)[:, :, 0:NTOK],
                                        AX, ALU.max, negate=True).then_inc(max_ready[g], 1)

                def keep_max(l, g):
                    for s in slots_of(g):
                        dve.wait_ge(max_placed[g], nth(attns, l, s))
                        v.tensor_copy(maxT[s][:, :], pair_in(s, 0)).then_inc(maxT_ready[g], 1)

                def invert_sums(l, g):
                    for s in slots_of(g):
                        dve.wait_ge(summed[g], nth(attns, l, s))
                        v.reciprocal(yT[s][:, 0:NTOK], bank(s, 1)[:, 0:NTOK]).then_inc(den_ready[g], 1)

                def normalise(l, g):
                    for s in slots_of(g):
                        dve.wait_ge(den_ready[g], nth(attns, l, s))
                        dve.wait_ge(attended[g], nth(attns, l, s))
                        v.tensor_tensor(oT[s][:, :], bank(s, 0)[:, 0:NTOK], yT[s][:, 0:NTOK],
                                        ALU.mult).then_inc(oT_ready[g], 1)

                def add_tokens(s, dst, j):
                    for t, (_, m) in enumerate(TILES):
                        last = v.tensor_tensor(dst[s][0:m, t, :], bank(s, j)[0:m, t * D:(t + 1) * D],
                                               dst[s][0:m, t, :], ALU.add)
                    return last

                def add_attention(l, g):
                    for s in slots_of(g):
                        if l < LAYERS:
                            dve.wait_ge(bias_added[g], nth(layers, l, s))
                        dve.wait_ge(proj_ready[g], nth(attns, l, s))
                        add_tokens(s, h if l < LAYERS else hh, 0).then_inc(attn_added[g], 1)

                def add_mlp(l, g):
                    for s in slots_of(g):
                        dve.wait_ge(mlp_bias[g], nth(layers, l, s))
                        dve.wait_ge(down_ready[g], nth(layers, l, s))
                        add_tokens(s, h, 1).then_inc(mlp_added[g], 1)

                def final_scale(l, g):
                    for s in slots_of(g):
                        dve.wait_ge(normed[g], nth(norms, N_FINAL, s))
                        for t, (_, m) in enumerate(TILES):
                            last = v.tensor_tensor(h[s][0:m, t, :], yn[s][0:m, t, :], cw[0:m, C_NW:C_NW + D],
                                                   ALU.mult)
                        last.then_inc(scaled_tok[g], 1)
                    for s in slots_of(g):
                        dve.wait_ge(scaled_tok[g], nth(twice, 0, s))
                        for t, (_, m) in enumerate(TILES):
                            last = v.tensor_tensor(h[s][0:m, t, :], h[s][0:m, t, :], cw[0:m, C_NB:C_NB + D], ALU.add)
                        last.then_inc(scaled_tok[g], 1)

                def ret_keep_v(l, g):
                    for s in slots_of(g):
                        dve.wait_ge(ret_qkv[g], nth(once, 0, s))
                        for t, (_, m) in enumerate(TILES):
                            last = v.tensor_copy(yn[s][0:m, t, :], bank(s, 1)[0:m, t * D:(t + 1) * D])
                        last.then_inc(ret_v[g], 1)

                def ret_weigh(l, g):
                    for s in slots_of(g):
                        dve.wait_ge(ret_scored[g], nth(once, 0, s))
                        for t, (_, m) in enumerate(TILES):
                            last = v.tensor_tensor(work[s][0:m, 1, t * NPAD:t * NPAD + NTOK],
                                                   bank(s, 0)[0:m, t * NPAD:t * NPAD + NTOK], decay_t[0:m, t, 0:NTOK],
                                                   ALU.mult)
                        last.then_inc(ret_weighted[g], 1)

                def ret_add(l, g):
                    for s in slots_of(g):
                        dve.wait_ge(ret_ready[g], nth(once, 0, s))
                        for t, (_, m) in enumerate(TILES):
                            last = v.scalar_tensor_tensor(h[s][0:m, t, :], bank(s, 0)[0:m, t * D:(t + 1) * D],
                                                          cw[0:m, C_SCALE:C_SCALE + 1], h[s][0:m, t, :],
                                                          ALU.mult, ALU.add)
                        last.then_inc(ret_added[g], 1)

                def route(l, g):
                    def link(k, s, ins):
                        ins.then_inc(routing[g], 1)

                    def linked(k, s):
                        dve.wait_ge(routing[g], nth(routes, k, s))

                    for s in slots_of(g):
                        dve.wait_ge(logits_ready[g], nth(once, 0, s))
                        for t, (_, m) in enumerate(TILES):
                            last = v.tensor_copy(logit[s][0:m, t, :], bank(s, 1)[0:m, t * EXPERTS:(t + 1) * EXPERTS])
                        link(0, s, last)
                    for s in slots_of(g):
                        linked(0, s)
                        v.memset(carrier[:, 12 + s:13 + s], 0.0)
                        for t in range(2):
                            last = v.max(top[s][:, t, :], logit[s][:, t, :])
                        link(1, s, last)
                    for s in slots_of(g):
                        linked(1, s)
                        v.tensor_tensor(gap[s][:, :], top[s][:, :, 1], top[s][:, :, 0],
                                        ALU.subtract).then_inc(gap_ready[g], 1)
                        for t in range(2):
                            last = v.max_index(topi[s][:, t, :], top[s][:, t, :], logit[s][:, t, :])
                        link(2, s, last)
                    for s in slots_of(g):
                        linked(2, s)
                        link(3, s, v.tensor_copy(topf[s][:, :, :], topi[s][:, :, 0:2]))
                    for s in slots_of(g):
                        dve.wait_ge(second_ready[g], nth(once, 0, s))
                        link(4, s, v.tensor_scalar(den[s][:, :], second[s][:, :], 1.0, None, ALU.add))
                    for s in slots_of(g):
                        linked(4, s)
                        link(5, s, v.reciprocal(gate[s][:, :, 0], den[s][:, :]))
                    for s in slots_of(g):
                        linked(5, s)
                        link(6, s, v.tensor_tensor(gate[s][:, :, 1], gate[s][:, :, 0], second[s][:, :], ALU.mult))
                    for s in slots_of(g):
                        linked(6, s)
                        for dst, k in ((gates2, 1), (gates, 0)):
                            for t in range(2):
                                last = v.tensor_scalar(dst[s][:, t, :], expert_f[:, :], topf[s][:, t, k:k + 1],
                                                       gate[s][:, t, k:k + 1], ALU.is_equal, ALU.mult)
                        link(7, s, last)
                    for s in slots_of(g):
                        linked(7, s)
                        link(8, s, v.tensor_tensor(gates[s][:, :, :], gates[s][:, :, :], gates2[s][:, :, :], ALU.add))
                    for s in slots_of(g):
                        linked(8, s)
                        dve.wait_ge(sum_ready[g], nth(once, 0, s))
                        v.memset(carrier[:, 16 + s:17 + s], 0.0).then_inc(ex_added[g], 1)

                part = {
                    "embed": embed, "embed_turn": embed_turn, "stat": stat,
                    "norm": lambda l, g: apply(g, h, yn, 2 * l), "split": split,
                    "stack0": lambda l, g: keep_k(l, g, 0), "stack1": lambda l, g: keep_k(l, g, 1),
                    **{f"rows{n}": lambda l, g, n=n: maxima(l, g, n) for n in range(8)},
                    "place": keep_max, "invert": invert_sums, "normalise": normalise, "add": add_attention,
                    "stat2": lambda l, g: moments_of(g, h, 2 * l + 1, attn_added, (attns, l)),
                    "norm2": lambda l, g: apply(g, h, yn, 2 * l + 1), "add2": add_mlp,
                    "final_stat": lambda l, g: moments_of(g, h, N_FINAL, mlp_added, (layers, LAYERS - 1)),
                    "final_norm": lambda l, g: apply(g, h, yn, N_FINAL), "final_scale": final_scale,
                    "ret_stat": lambda l, g: moments_of(g, h, N_RET, scaled_tok, (twice, 1)),
                    "ret_norm": lambda l, g: apply(g, h, yn, N_RET), "ret_proj": ret_keep_v, "ret_scores": ret_weigh,
                    "ret_out": ret_add, "x_stat": lambda l, g: moments_of(g, h, N_X, ret_added, (once, 0)),
                    "x_norm": lambda l, g: apply(g, h, hh, N_X),
                    "rms1_stat": lambda l, g: moments_of(g, hh, N_RMS1, normed, (norms, N_X), rms=True),
                    "rms1_norm": lambda l, g: apply(g, hh, yn, N_RMS1, rms=True), "rope_proj": rope_rotate,
                    "rope_turn": rope_values,
                    "rms2_stat": lambda l, g: moments_of(g, hh, N_RMS2, attn_added, (attns, ROPE), rms=True),
                    "rms2_norm": lambda l, g: apply(g, hh, yn, N_RMS2, rms=True), "route": route,
                }
                for name, l, g in SCHEDULE:
                    if name in part:
                        part[name](l, g)

                with dve.Fori(0, EXPERTS) as e:
                    expert = dve.snap((i * EXPERTS + e) * 2)
                    added = dve.snap((i * (EXPERTS + 1) + e) * 2)
                    for s in SLOTS:
                        dve.wait_ge(ex_added[s // 2], nth(added, 0, s))
                        dve.wait_ge(ex_down[s // 2], nth(expert, 0, s))
                        for t, (_, m) in enumerate(TILES):
                            last = v.scalar_tensor_tensor(h[s][0:m, t, :], bank(s, 0)[0:m, t * D:(t + 1) * D],
                                                          gates[s][0:m, t, bass.ds(e, 1)], h[s][0:m, t, :],
                                                          ALU.mult, ALU.add)
                        last.then_inc(ex_added[s // 2], 1)


def columns(*parts):
    return np.ascontiguousarray(np.concatenate([np.asarray(p, np.float32).reshape(P, -1) for p in parts], axis=1))


def swapped(w):
    return np.asarray(w).reshape(D, D // 2, 2)[:, :, ::-1].reshape(D, D)


def rope_tables():
    inv = (1.0 / np.float32(10000.0) ** (np.arange(0, HD, 2, dtype=np.float32) / np.float32(HD))).astype(np.float32)
    ang = np.arange(NPAD, dtype=np.float32)[:, None] * inv[None, :]
    cos, sin = np.zeros((HD, NPAD), np.float32), np.zeros((HD, NPAD), np.float32)
    cos[0::2], cos[1::2] = np.cos(ang).T, np.cos(ang).T
    sin[0::2], sin[1::2] = -np.sin(ang).T, np.sin(ang).T
    return [np.tile(a, (HEADS, 1)) for a in (cos, sin)]


def selections():
    out = np.zeros((P, 4, NPAIR, P), np.float32)
    d = np.arange(HD)
    for n, places in enumerate(((0, 2), (1,), (0, 1), (2,))):
        for u in range(NPAIR):
            for par in range(2):
                for r in places:
                    out[(2 * u + par) * HD + d, n, u, 64 * par + r * HD + d] = 1.0
    return out.reshape(P, -1)


def kernel(**inputs):
    import concourse.bacc as bacc
    from concourse.bass_utils import run_bass_kernel_spmd

    a = {k: np.asarray(v) for k, v in inputs.items()}

    def rows(v):
        return np.broadcast_to(np.asarray(v).reshape(1, -1), (P, np.asarray(v).size))

    tower = []
    for l in range(LAYERS):
        w, b = a["L0_tok_qkv_w"][l], a["L0_tok_qkv_b"][l]
        tower.append(columns(
            w[:, 0:D], w[:, D:2 * D], w[:, 2 * D:3 * D], a["L0_tok_proj_w"][l], a["L0_tok_fc1_w"][l],
            a["L0_tok_fc2_w"][l].reshape(HC, P, D).transpose(1, 0, 2), rows(b[2 * D:3 * D]),
            rows(a["L0_tok_proj_b"][l]), rows(a["L0_tok_fc2_b"][l]), a["L0_tok_ln1_w"][l], a["L0_tok_ln1_b"][l],
            a["L0_tok_ln2_w"][l], a["L0_tok_ln2_b"][l], b[0:D], b[D:2 * D], a["L0_tok_fc1_b"][l].reshape(HC, P).T))
    conv = np.zeros((P, HALF, D), np.float32)
    cv = a["L0_tok_conv_w"].reshape(XROWS, PATCH, D)
    conv[0:XROWS] = cv[:, 0:HALF]
    conv[XSHIFT:XSHIFT + XROWS] = cv[:, HALF:PATCH]
    const_w = columns(
        conv, a["L0_ffn_wq"], swapped(a["L0_ffn_wq"]), a["L0_ffn_wk"], swapped(a["L0_ffn_wk"]), a["L0_ffn_wv"],
        a["L0_ffn_wo"], a["L0_attn_Wq"].T, a["L0_attn_Wk"].T, a["L0_attn_Wv"].T, a["L0_attn_Wo"].T,
        a["L0_ffn_router_w"], rows(a["L0_tok_norm_w"]), rows(a["L0_tok_norm_b"]), a["L0_tok_pos_embed"][0].T,
        *rope_tables(), a["L0_ffn_attn_norm_w"], a["L0_ffn_ffn_norm_w"], a["L0_tok_conv_b"], a["L0_tok_cls_token"],
        rows(a["L0_attn_decay_logit"]), rows(a["L0_attn_out_scale"]))
    tower_w = np.ascontiguousarray(np.stack(tower, axis=1))
    assert const_w.shape[1] == C_N and tower_w.shape == (P, LAYERS, L_N)
    arrays = {"x": a["x"], "tower_w": tower_w, "const_w": const_w, "sel_w": selections(),
              "w1": a["L0_ffn_w1"], "w2": a["L0_ffn_w2"]}
    nc = bacc.Bacc("TRN2", target_bir_lowering=False, num_devices=1)
    args = [nc.dram_tensor(n, v.shape, mybir.dt.from_np(v.dtype), kind="ExternalInput").ap() for n, v in arrays.items()]
    out = nc.dram_tensor("out", (B, NTOK, D), F32, kind="ExternalOutput").ap()
    build(nc, *args, out)
    r = run_bass_kernel_spmd(nc, [arrays], core_ids=[0])
    return r.results[0]["out"]
```
